# Optimizing a Trainium2 kernel written in Bass

```python
import numpy as np
import jax
import jax.numpy as jnp

def _softmax(x, axis=-1):
    return jax.nn.softmax(x, axis=axis)

def _gelu(x):
    return jax.nn.gelu(x, approximate=True)

def _silu(x):
    return jax.nn.silu(x)

def _sigmoid(x):
    return jax.nn.sigmoid(x)

def _layernorm(x, axis=-1, eps=1e-05):
    m = jnp.mean(x, axis=axis, keepdims=True)
    v = jnp.var(x, axis=axis, keepdims=True)
    return (x - m) / jnp.sqrt(v + eps)

def _scatter_add(tgt, idx, src, axis=0):
    return tgt.at[idx].add(src)

def _segment_sum(src, seg, n):
    return jax.ops.segment_sum(src, seg, n)
kernel_name = 'mk_flamingo_gated_d1_seqx_r8_a6b4cd'

def setup_inputs(seed: int=0):
    np.random.seed(seed)
    _w = jnp.asarray

    def _rec_inputs():
        import jax
        import jax.numpy as jnp
        _rk = jax.random.key(seed)
        x = 7.22e-05 + 1 * jax.random.normal(jax.random.fold_in(_rk, 1), (2, 512, 128), jnp.float32)
        _lenS = 512 - jax.random.randint(jax.random.fold_in(_rk, 7), (2,), 0, max(1, 512 // 4) + 1, jnp.int32)
        _lenS2 = 77 - jax.random.randint(jax.random.fold_in(_rk, 8), (2,), 0, max(1, 77 // 4) + 1, jnp.int32)
        _ctx_1024P = jax.random.normal(jax.random.fold_in(_rk, 11), (2, 16, 128), jnp.float32)
        _ctx_1024c = jax.random.dirichlet(jax.random.fold_in(_rk, 511), 0.3 * jnp.ones((16,), jnp.float32), (2, 77))
        _ctx_1024t = jnp.einsum('bsk,bkd->bsd', _ctx_1024c, _ctx_1024P)
        _ctx_1024t = _ctx_1024t * jax.lax.rsqrt(jnp.mean(jnp.square(_ctx_1024t)) + 1e-12) * 0.953939
        ctx_1024 = -1.39393e-06 + 0.999914 * (_ctx_1024t + 0.3 * jax.random.normal(jax.random.fold_in(_rk, 611), (2, 77, 128), jnp.float32))
        _g = jax.random.normal(jax.random.fold_in(_rk, 9001), (2, 1), jnp.float32)
        _g = jnp.sign(_g) * jnp.maximum(jnp.abs(_g), 1.0) + (_g == 0) * 1.0
        g_xattn = _g[0]
        g_ffn = _g[1]
        return (x, ctx_1024, g_xattn, g_ffn)
    x, ctx_1024, g_xattn, g_ffn = _rec_inputs()

    def _L0_xattn_setup():
        import jax, jax.numpy as jnp
        import numpy as np
        DIM = 128
        CTX_DIM = 128
        HEADS = 16
        DIM_HEAD = 64
        INNER = HEADS * DIM_HEAD
        FF_INNER = 4 * DIM
        EPS = 1e-05

        def layer_norm(x, g, b):
            mu = jnp.mean(x, axis=-1, keepdims=True)
            var = jnp.var(x, axis=-1, keepdims=True)
            return (x - mu) * jax.lax.rsqrt(var + EPS) * g + b
        key = jax.random.key(seed)
        ks = jax.random.split(key, 9)
        b, n, j = (4, 256, 128)
        inp = {'x': jax.random.normal(ks[0], (b, n, DIM), dtype=jnp.float32), 'context': jax.random.normal(ks[1], (b, j, CTX_DIM), dtype=jnp.float32), 'ln_g': jnp.ones((DIM,), jnp.float32), 'ln_b': jnp.zeros((DIM,), jnp.float32), 'cln_g': jnp.ones((CTX_DIM,), jnp.float32), 'cln_b': jnp.zeros((CTX_DIM,), jnp.float32), 'Wq': jax.random.normal(ks[2], (DIM, INNER), dtype=jnp.float32) * DIM ** (-0.5), 'Wkv': jax.random.normal(ks[3], (CTX_DIM, 2 * DIM_HEAD), dtype=jnp.float32) * CTX_DIM ** (-0.5), 'Wo': jax.random.normal(ks[4], (INNER, DIM), dtype=jnp.float32) * INNER ** (-0.5), 'Wff1': jax.random.normal(ks[5], (DIM, 2 * FF_INNER), dtype=jnp.float32) * DIM ** (-0.5), 'Wff2': jax.random.normal(ks[6], (FF_INNER, DIM), dtype=jnp.float32) * FF_INNER ** (-0.5)}
        return inp
    _L0_xattn_all = _L0_xattn_setup()
    _L0_xattn_in = {k: v for k, v in _L0_xattn_all.items() if k in ('ln_g', 'ln_b', 'cln_g', 'cln_b', 'Wq', 'Wkv', 'Wo', 'Wff1', 'Wff2')}
    del _L0_xattn_all

    def _L0_ffn_setup():
        import jax, jax.numpy as jnp
        import numpy as np
        HIDDEN = 128
        FFN = 512
        NUM_EXPERTS = 8
        TOP_K = 2
        BATCH, SEQ = (2, 256)
        key = jax.random.key(seed)
        ks = jax.random.split(key, 6)
        s_h = 1.0 / np.sqrt(HIDDEN)
        s_f = 1.0 / np.sqrt(FFN)
        return {'hidden_states': jax.random.normal(ks[0], (BATCH, SEQ, HIDDEN), jnp.float32), 'gate_w': jax.random.uniform(ks[1], (HIDDEN, NUM_EXPERTS), jnp.float32, -s_h, s_h), 'gate_b': jax.random.uniform(ks[2], (NUM_EXPERTS,), jnp.float32, -s_h, s_h), 'w1': jax.random.uniform(ks[3], (NUM_EXPERTS, HIDDEN, FFN), jnp.float32, -s_h, s_h), 'w3': jax.random.uniform(ks[4], (NUM_EXPERTS, HIDDEN, FFN), jnp.float32, -s_h, s_h), 'w2': jax.random.uniform(ks[5], (NUM_EXPERTS, FFN, HIDDEN), jnp.float32, -s_f, s_f)}
    _L0_ffn_all = _L0_ffn_setup()
    _L0_ffn_in = {k: v for k, v in _L0_ffn_all.items() if k in ('gate_w', 'gate_b', 'w1', 'w3', 'w2')}
    del _L0_ffn_all
    return {'x': x, 'ctx_1024': ctx_1024, 'g_xattn': g_xattn, 'g_ffn': g_ffn, 'L0_xattn_ln_g': _L0_xattn_in['ln_g'], 'L0_xattn_ln_b': _L0_xattn_in['ln_b'], 'L0_xattn_cln_g': _L0_xattn_in['cln_g'], 'L0_xattn_cln_b': _L0_xattn_in['cln_b'], 'L0_xattn_Wq': _L0_xattn_in['Wq'], 'L0_xattn_Wkv': _L0_xattn_in['Wkv'], 'L0_xattn_Wo': _L0_xattn_in['Wo'], 'L0_xattn_Wff1': _L0_xattn_in['Wff1'], 'L0_xattn_Wff2': _L0_xattn_in['Wff2'], 'L0_ffn_gate_w': _L0_ffn_in['gate_w'], 'L0_ffn_gate_b': _L0_ffn_in['gate_b'], 'L0_ffn_w1': _L0_ffn_in['w1'], 'L0_ffn_w3': _L0_ffn_in['w3'], 'L0_ffn_w2': _L0_ffn_in['w2']}

def reference(x, ctx_1024, g_xattn, g_ffn, L0_xattn_ln_g, L0_xattn_ln_b, L0_xattn_cln_g, L0_xattn_cln_b, L0_xattn_Wq, L0_xattn_Wkv, L0_xattn_Wo, L0_xattn_Wff1, L0_xattn_Wff2, L0_ffn_gate_w, L0_ffn_gate_b, L0_ffn_w1, L0_ffn_w3, L0_ffn_w2):
    import jax
    import jax.numpy as jnp

    def _L0_xattn_ref(x, context, ln_g, ln_b, cln_g, cln_b, Wq, Wkv, Wo, Wff1, Wff2):
        import jax, jax.numpy as jnp
        import numpy as np
        DIM = 128
        CTX_DIM = 128
        HEADS = 16
        DIM_HEAD = 64
        INNER = HEADS * DIM_HEAD
        FF_INNER = 4 * DIM
        EPS = 1e-05

        def layer_norm(x, g, b):
            mu = jnp.mean(x, axis=-1, keepdims=True)
            var = jnp.var(x, axis=-1, keepdims=True)
            return (x - mu) * jax.lax.rsqrt(var + EPS) * g + b
        scale = DIM_HEAD ** (-0.5)
        xn = layer_norm(x, ln_g, ln_b)
        cn = layer_norm(context, cln_g, cln_b)
        b, n, _ = xn.shape
        q = (xn @ Wq).reshape(b, n, HEADS, DIM_HEAD).transpose(0, 2, 1, 3) * scale
        kv = cn @ Wkv
        k, v = (kv[..., :DIM_HEAD], kv[..., DIM_HEAD:])
        sim = jnp.einsum('bhid,bjd->bhij', q, k)
        attn = jax.nn.softmax(sim, axis=-1)
        out = jnp.einsum('bhij,bjd->bhid', attn, v)
        out = out.transpose(0, 2, 1, 3).reshape(b, n, INNER) @ Wo
        ff = xn @ Wff1
        h, gate = (ff[..., :FF_INNER], ff[..., FF_INNER:])
        out = out + jax.nn.silu(gate) * h @ Wff2
        return out

    def _L0_ffn_ref(hidden_states, gate_w, gate_b, w1, w3, w2):
        import jax, jax.numpy as jnp
        import numpy as np
        HIDDEN = 128
        FFN = 512
        NUM_EXPERTS = 8
        TOP_K = 2
        BATCH, SEQ = (2, 256)
        B, S, D = hidden_states.shape
        T = B * S
        x = hidden_states.reshape(T, D)
        logits = x @ gate_w + gate_b
        probs = jax.nn.softmax(logits.astype(jnp.float32), axis=-1)
        top_w, top_idx = jax.lax.top_k(probs, TOP_K)
        top_w = top_w / jnp.sum(top_w, axis=-1, keepdims=True)
        combine = jnp.zeros((T, NUM_EXPERTS), jnp.float32)
        combine = combine.at[jnp.arange(T)[:, None], top_idx].set(top_w)
        combine = combine.astype(x.dtype)
        h = jax.nn.silu(jnp.einsum('td,edf->tef', x, w1)) * jnp.einsum('td,edf->tef', x, w3)
        out_e = jnp.einsum('tef,efd->ted', h, w2)
        out = jnp.einsum('ted,te->td', out_e, combine)
        return out.reshape(B, S, D)
    x = x + jnp.tanh(g_xattn[0]) * _L0_xattn_ref(_layernorm(x, axis=-1), ctx_1024, L0_xattn_ln_g, L0_xattn_ln_b, L0_xattn_cln_g, L0_xattn_cln_b, L0_xattn_Wq, L0_xattn_Wkv, L0_xattn_Wo, L0_xattn_Wff1, L0_xattn_Wff2)
    x = x + jnp.tanh(g_ffn[0]) * _L0_ffn_ref(_layernorm(x, axis=-1), L0_ffn_gate_w, L0_ffn_gate_b, L0_ffn_w1, L0_ffn_w3, L0_ffn_w2)
    return x

_drawn_inputs = setup_inputs


def setup_inputs(seed=0):
    import zlib

    import numpy as np

    out = dict(_drawn_inputs(seed))
    spreads = {'L0_xattn_ln_g': (1.0, 0.2),
     'L0_xattn_ln_b': (0.0, 0.1),
     'L0_xattn_cln_g': (1.0, 0.2),
     'L0_xattn_cln_b': (0.0, 0.1)}
    factors = {'L0_ffn_gate_b': 3.798}
    for name, (base, spread) in spreads.items():
        noise = np.random.default_rng([zlib.crc32(name.encode()), seed]).standard_normal(out[name].shape)
        drawn = base * np.exp(spread * noise) if base else spread * noise
        out[name] = jnp.asarray(drawn.astype(out[name].dtype))
    for name, factor in factors.items():
        out[name] = (out[name] * factor).astype(out[name].dtype)
    return out
```

```python
from contextlib import ExitStack

import concourse.bass as bass
from concourse import mybir

ALU = mybir.AluOpType
ACT = mybir.ActivationFunctionType
AX_X = mybir.AxisListType.X
F32 = mybir.dt.float32
F32R = mybir.dt.float32r
BF16 = mybir.dt.bfloat16
U32 = mybir.dt.uint32
I32 = mybir.dt.int32
P = 128


class Steps:

    def __init__(self, engine, semaphore):
        self.engine, self.semaphore, self.count, self.shift = engine, semaphore, 0, 0

    def link(self, instruction):
        self.did(instruction)
        self.wait()

    def drained(self, instruction):
        self.engine.drain()

    def did(self, instruction):
        instruction.then_inc(self.semaphore, 1)
        self.count += 1

    def wait(self):
        self.engine.wait_ge(self.semaphore, self.count + self.shift)

    def enter(self, turn, first, per_turn):
        self.begin, self.per_turn = self.count, per_turn
        self.shift = (turn - first) * per_turn

    def leave(self, turns):
        assert self.count - self.begin == self.per_turn, (self.count - self.begin, self.per_turn)
        self.count, self.shift = self.begin + turns * self.per_turn, 0


def gated_block_kernel(nc, x, ctx_in, g_xattn, g_ffn, ln_g, ln_b, cln_g, cln_b, wq, wkv, wo, wff1, wff2,
                       gate_w, gate_b, w1, w3, w2, out):
    B, N, D = x.shape
    J = ctx_in.shape[1]
    INNER = wq.shape[1]
    DH = wkv.shape[1] // 2
    H = INNER // DH
    FF = wff2.shape[0]
    E, _, F = w1.shape
    EPS = 1e-5
    TILES = B * N // P
    PER_BATCH = N // P
    HJ = H * J
    PAIRS = H // 2
    CH = -(-HJ // P)
    LASTC = HJ - (CH - 1) * P
    HB = 6
    TAILH = H - 2 * HB
    FC = F // P
    CAP = TILES * P
    SLOT_TILES = (2 * B * N - E) // P + E
    SPARE = SLOT_TILES - 2 * B * N // P
    REGION = E * CAP + SPARE * P
    ROW = D + 2
    RETURN = 2 * B * N
    assert D == P and 2 * DH == P and F == 4 * P and FF == 4 * P and HB * J <= 512 and TILES % 2 == 0

    dispatched = nc.dram_tensor("dispatched", (REGION, ROW), F32, kind="Internal").ap()
    returned = nc.dram_tensor("returned", (RETURN, D), F32, kind="Internal").ap()

    with ExitStack() as ctx:
        def sb(name, shape, dt=F32):
            return ctx.enter_context(nc.sbuf_tensor(name, shape, dt))

        def sem(name):
            return ctx.enter_context(nc.semaphore(name))

        X = sb("X", [P, TILES, D])
        X2 = sb("X2", [P, TILES, D])
        CTX = sb("CTX", [J, B, D])
        CHAT = sb("CHAT", [J, B, D])
        CN = sb("CN", [P, B * J])
        WKV2 = sb("WKV2", [P, 2, 2, DH])
        kdiag = sb("kdiag", [P, B, 2, J])
        VP = P + 2 * J + P
        vpad = sb("vpad", [P, B, VP])
        early = sb("early", [P, 2 * INNER])
        WQ = early[:, 0:INNER]
        WQT = early[:, INNER:2 * INNER].rearrange("p (q d) -> p q d", d=D)
        PT = early[:, 0:CH * P].rearrange("p (q d) -> p q d", d=P)
        HT = early[:, CH * P:CH * P + FF].rearrange("p (q d) -> p q d", d=P)
        PR = sb("PR", [P, 2, HJ])
        F1 = PR[:, 0, 0:2 * FF]
        WO = PR[:, 1, 0:INNER].rearrange("p (q d) -> p q d", d=D)
        SG = PR[:, :, 0:F]
        A_hi = sb("A_hi", [P, B, HJ], F32R)
        A_lo = sb("A_lo", [P, B, HJ], F32R)
        VO = sb("VO", [P, B, CH, D])
        F1_hi = sb("F1_hi", [P, 2 * FF], F32R)
        F1_lo = sb("F1_lo", [P, 2 * FF], F32R)
        F2 = sb("F2", [P, FF // P, D])
        lng = sb("lng", [P, 4])
        gates = sb("gates", [P, 2])
        tg = sb("tg", [P, 2])
        GW = sb("GW", [P, E])
        GB = sb("GB", [P, E])
        half = sb("half", [P, TILES])
        stats = sb("stats", [P, TILES, 6])
        mv = sb("mv", [P, TILES, 2])
        veps = sb("veps", [P, TILES])
        rx = sb("rx", [P, TILES])
        cstats = sb("cstats", [J, B, 6])
        cmv = sb("cmv", [J, B, 2])
        cveps = sb("cveps", [J, B])
        rc = sb("rc", [J, B])
        identf = sb("identf", [P, P])
        ones_b = sb("ones_b", [P, P], BF16)
        lower_b = sb("lower_b", [P, P], BF16)
        iota_e = sb("iota_e", [P, E])
        base_e = sb("base_e", [P, E])
        dest = sb("dest", [P, TILES, 2], U32)
        padrow = sb("padrow", [P, ROW])
        XH = sb("XH", [P, 2, D])
        XN = sb("XN", [P, 2, P])
        XN_hi = [sb(f"XN_hi{u}", [P, P], F32R) for u in range(2)]
        XN_lo = [sb(f"XN_lo{u}", [P, P], F32R) for u in range(2)]
        M16 = sb("M16", [P, H])
        RS = sb("RS", [P, 2, H])
        RI = sb("RI", [P, 2, H])
        TH = sb("TH", [P, FF])
        HH = sb("HH", [P, 2, FF])
        st2 = sb("st2", [P, 6])
        mv2 = sb("mv2", [P, 2])
        ve2 = sb("ve2", [P, 1])
        r2 = sb("r2", [P, 1])
        YB = sb("YB", [P, 2, D])
        YT = sb("YT", [P, P])
        rows = sb("rows", [P, TILES, 2, ROW])
        LG = sb("LG", [P, E])
        MX = sb("MX", [P, 8])
        IX = sb("IX", [P, 8], U32)
        IXF = sb("IXF", [P, 2])
        gap = sb("gap", [P, 1])
        eg = sb("eg", [P, 1])
        wsum = sb("wsum", [P, 1])
        wone = sb("wone", [P, 1])
        pick = sb("pick", [P, 2, E])
        Ms = sb("Ms", [P, E], BF16)
        Macc = sb("Macc", [P, TILES + 1, E], BF16)
        rkb = sb("rkb", [P, E])
        prod = sb("prod", [P, 2, E])
        slot = sb("slot", [P, TILES, 2], U32)
        T8 = sb("T8", [1, E])
        T8u = sb("T8u", [1, E], U32)
        Tn = sb("Tn", [1, E])
        tri = sb("tri", [1, E, E])
        TT = sb("TT", [1, E, E])
        Tend = sb("Tend", [1, E])
        iota_s = sb("iota_s", [1, SLOT_TILES])
        GE = sb("GE", [1, SLOT_TILES, E])
        GT = sb("GT", [1, SLOT_TILES, E])
        es = sb("es", [1, SLOT_TILES])
        ts_ = sb("ts_", [1, SLOT_TILES])
        rowb = sb("rowb", [1, SLOT_TILES])
        expert_of = sb("expert_of", [1, SLOT_TILES], I32)
        row_of = sb("row_of", [1, SLOT_TILES], I32)
        WS = sb("WS", [P, 2, 3 * F])
        W13_hi = sb("W13_hi", [P, E, 2 * F], F32R)
        W13_lo = sb("W13_lo", [P, E, 2 * F], F32R)
        W2_hi = sb("W2_hi", [P, E, F], F32R)
        W2_lo = sb("W2_lo", [P, E, F], F32R)
        RIN = 4
        RT = WS[:, 0, 0:RIN * ROW].rearrange("p (k c) -> p k c", c=ROW)
        XT_hi, XT_lo = XN_hi, XN_lo
        HE = HH
        HT_hi = F1_hi[:, 0:F].rearrange("p (q d) -> p q d", d=P)
        HT_lo = F1_lo[:, 0:F].rearrange("p (q d) -> p q d", d=P)
        YO = XH
        back = rows[:, :, :, :].rearrange("p t k c -> p (t k c)")[:, 0:TILES * 2 * D].rearrange(
            "p (t c) -> p t c", c=2 * D)

        bank = [ctx.enter_context(nc.psum_tensor(f"bank{i}", [P, 512], F32)) for i in range(8)]
        SC, GP, UP, TP, SM = bank[0:3], bank[3], bank[4], bank[5:7], bank[7]
        xh_T, acc_ps, y_T = GP[:, 0:P], SM[:, P:2 * P], SM[:, 2 * P:3 * P]
        lg_ps, rk_ps, ct_ps = SM[:, 384:384 + E], SM[:, 400:400 + E], SM[0:1, 416:416 + E]

        ld_ctx, ld_x, ld_wkv, ld_vec, ld_gate = sem("ld_ctx"), sem("ld_x"), sem("ld_wkv"), sem("ld_vec"), sem("ld_gate")
        ld_wq, ld_wo, ld_f1, ld_f2, ld_gw = sem("ld_wq"), sem("ld_wo"), sem("ld_f1"), sem("ld_f2"), sem("ld_gw")
        ld_ws = [sem(f"ld_ws{u}") for u in range(2)]
        regions_blank = sem("regions_blank")
        consts = sem("consts")
        ident_zero = sem("ident_zero")
        cvar_ready, crs_ready, chat_ready = sem("cvar_ready"), sem("crs_ready"), sem("chat_ready")
        xvar_ready, xrs_ready = sem("xvar_ready"), sem("xrs_ready")
        cT_ready, cn_ready, kv_ready, kv_used = sem("cT_ready"), sem("cn_ready"), sem("kv_ready"), sem("kv_used")
        diag_zero = sem("diag_zero")
        wqT_ready, wqT_used = sem("wqT_ready"), sem("wqT_used")
        a_ready, ahi_ready, a_used = sem("a_ready"), sem("ahi_ready"), sem("a_used")
        vo_ready, vo_used = sem("vo_ready"), sem("vo_used")
        f1hi_ready, f1_split = sem("f1hi_ready"), sem("f1_split")
        tg_ready = sem("tg_ready")
        xh_ready, xT_ready, xn_ready, xn_split = sem("xh_ready"), sem("xT_ready"), sem("xn_ready"), sem("xn_split")
        scores_ready, shift_ready, exp_ready = sem("scores_ready"), sem("shift_ready"), sem("exp_ready")
        rsum_ready, probs_ready = sem("rsum_ready"), sem("probs_ready")
        gu_ready, tanh_ready, h_ready = sem("gu_ready"), sem("tanh_ready"), sem("h_ready")
        tp_ready, tp_copied = sem("tp_ready"), sem("tp_copied")
        acc_ready, var2_ready, r2_ready, y_ready = sem("acc_ready"), sem("var2_ready"), sem("r2_ready"), sem("y_ready")
        yT_ready, yT_copied, row_copied = sem("yT_ready"), sem("yT_copied"), sem("row_copied")
        logits_ready, gap_ready, eg_ready = sem("logits_ready"), sem("gap_ready"), sem("eg_ready")
        picks_ready, rank_ready, slots_ready = sem("picks_ready"), sem("rank_ready"), sem("slots_ready")
        rank_read = sem("rank_read")
        weights_ready = sem("weights_ready")
        whi_ready, w_split = sem("whi_ready"), sem("w_split")
        rows_out = sem("rows_out")
        counts_ready, tables_ready = sem("counts_ready"), sem("tables_ready")
        rt_in = [sem(f"rt_in{k}") for k in range(RIN)]
        sT_ready, shi_ready, s_split = sem("sT_ready"), sem("shi_ready"), sem("s_split")
        sgate_ready, sup_ready, silu_ready, he_ready = sem("sgate_ready"), sem("sup_ready"), sem("silu_ready"), sem("he_ready")
        heT_ready, hthi_ready, ht_split = sem("heT_ready"), sem("hthi_ready"), sem("ht_split")
        ye_ready, yo_ready = sem("ye_ready"), sem("yo_ready")
        yo_out = [sem(f"yo_out{u}") for u in range(2)]
        back_in, osum_ready, out_done = sem("back_in"), sem("osum_ready"), sem("out_done")
        dve_steps = sem("dve_steps")
        pool_steps = sem("pool_steps")

        x_v = x.rearrange("b (t p) d -> p (b t) d", p=P)
        out_v = out.rearrange("b (t p) d -> p (b t) d", p=P)
        col = "(p a) -> p a"

        block = ctx.enter_context(nc.Block())

        @block.sync
        def _(sp):
            sp.dma_start(X[:, :, :], x_v).then_inc(ld_x, 16)
            sp.dma_start(WQ[:, :], wq).then_inc(ld_wq, 16)
            sp.dma_start(F1[:, :], wff1).then_inc(ld_f1, 16)
            sp.dma_start(WO[:, :, :], wo.rearrange("(q p) d -> p q d", p=P)).then_inc(ld_wo, 16)
            sp.dma_start(F2[:, :, :], wff2.rearrange("(q p) d -> p q d", p=P)).then_inc(ld_f2, 16)
            sp.wait_ge(consts, 1)
            sp.dma_start(dispatched.rearrange("(t p) c -> p t c", p=P),
                         padrow[:, :].unsqueeze(1).to_broadcast([P, REGION // P, ROW])).then_inc(regions_blank, 16)

            def load_expert(e, u):
                if not isinstance(e, int) or e >= 2:
                    sp.wait_ge(w_split, e - 1)
                sp.dma_start(WS[:, u, 0:F], w1[bass.ds(e, 1)].rearrange("a d f -> d (a f)")).then_inc(ld_ws[u], 16)
                sp.dma_start(WS[:, u, F:2 * F], w3[bass.ds(e, 1)].rearrange("a d f -> d (a f)")).then_inc(ld_ws[u], 16)
                sp.dma_start(WS[:, u, 2 * F:3 * F].rearrange("p (q d) -> p q d", d=D),
                             w2[bass.ds(e, 1)].rearrange("a (q p) d -> p (a q) d", p=P)).then_inc(ld_ws[u], 16)

            load_expert(0, 0)
            load_expert(1, 1)
            with sp.Fori(1, E // 2) as i:
                for u in range(2):
                    load_expert(2 * i + u, u)

            sp.wait_ge(tables_ready, 1)
            sp.wait_ge(w_split, E)
            sp.wait_ge(rows_out, 2 * TILES * 16)

            def load_slots(s, k):
                if not isinstance(s, int) or s >= RIN:
                    sp.wait_ge(yo_out[k % 2], ((s - RIN) // 2 + 1) * 16)
                row = sp.value_load(row_of[0:1, bass.ds(s, 1)], min_val=0, max_val=REGION - P)
                sp.dma_start(RT[:, k, :], dispatched[bass.ds(row, P), :]).then_inc(rt_in[k], 16)

            for s in range(RIN):
                load_slots(s, s)
            with sp.Fori(1, SLOT_TILES // RIN) as i:
                for k in range(RIN):
                    load_slots(RIN * i + k, k)
            for s in range(SLOT_TILES // RIN * RIN, SLOT_TILES):
                load_slots(s, s % RIN)

            sp.wait_ge(yo_out[0], (SLOT_TILES + 1) // 2 * 16)
            sp.wait_ge(yo_out[1], SLOT_TILES // 2 * 16)
            sp.dma_start(back, returned.rearrange("(t p k) d -> p t (k d)", p=P, k=2)).then_inc(back_in, 16)
            sp.wait_ge(osum_ready, 1)
            sp.dma_start(out_v, X2[:, :, :]).then_inc(out_done, 16)
            sp.wait_ge(out_done, 16)

        @block.gpsimd
        def _(gp):
            steps = Steps(gp, pool_steps)
            pad_ix = padrow[:, D:D + 1].bitcast(U32)
            nc.gpsimd.memset(padrow[:, 0:D], 0.0)
            nc.gpsimd.memset(padrow[:, D + 1:ROW], 0.0)
            steps.link(nc.gpsimd.iota(pad_ix, pattern=[[0, 1]], base=RETURN, channel_multiplier=0))
            nc.gpsimd.memset(half[:, :], -0.5).then_inc(consts, 1)
            steps.link(nc.gpsimd.memset(identf[:, :], 0.0))
            nc.gpsimd.affine_select(out=identf[:, :], in_=identf[:, :], compare_op=ALU.not_equal, fill=1.0,
                                    base=0, pattern=[[-1, P]], channel_multiplier=1).then_inc(consts, 1)
            gp.wait_ge(cvar_ready, 1)
            nc.gpsimd.tensor_tensor(rc[:, :], cveps[:, :], half[0:J, 0:B], ALU.pow).then_inc(crs_ready, 1)
            gp.wait_ge(xvar_ready, 1)
            nc.gpsimd.tensor_tensor(rx[:, :], veps[:, :], half[:, :], ALU.pow).then_inc(xrs_ready, 1)
            steps.link(nc.gpsimd.memset(ones_b[:, :], 1.0))
            nc.gpsimd.affine_select(out=lower_b[:, :], in_=ones_b[:, :], compare_op=ALU.is_gt, fill=0.0,
                                    base=0, pattern=[[1, P]], channel_multiplier=-1)
            nc.gpsimd.iota(iota_e[:, :], pattern=[[1, E]], base=0, channel_multiplier=0,
                           allow_small_or_imprecise_dtypes=True)
            nc.gpsimd.iota(base_e[:, :], pattern=[[CAP, E]], base=0, channel_multiplier=0,
                           allow_small_or_imprecise_dtypes=True)
            nc.gpsimd.iota(iota_s[:, :], pattern=[[1, SLOT_TILES]], base=0, channel_multiplier=0,
                           allow_small_or_imprecise_dtypes=True)
            nc.gpsimd.iota(dest[:, :, :], pattern=[[2 * P, TILES], [1, 2]], base=0, channel_multiplier=2)
            steps.link(nc.gpsimd.memset(tri[:, :, :], 1.0))
            steps.link(nc.gpsimd.affine_select(out=tri[:, :, :], in_=tri[:, :, :], compare_op=ALU.is_ge, fill=0.0,
                                               base=0, pattern=[[1, E], [-1, E]], channel_multiplier=0))
            steps.link(nc.gpsimd.memset(Macc[:, 0, :], 0.0))
            nc.gpsimd.tensor_copy(rows[:, :, :, D:D + 1].bitcast(U32).rearrange("p t k a -> p t (k a)"),
                                  dest[:, :, :]).then_inc(consts, 1)

            def normalise(t, u):
                gp.wait_ge(rsum_ready, t + 1)
                v = PR[:, u, :].rearrange("p (h j) -> p h j", j=J)
                nc.gpsimd.tensor_tensor(v, v, RI[:, u, :].unsqueeze(2).to_broadcast([P, H, J]),
                                        ALU.mult).then_inc(probs_ready, 1)

            def split_expert(e, u):
                gp.wait_ge(ld_ws[u], (e // 2 + 1) * 48)
                nc.gpsimd.tensor_copy(W13_hi[:, bass.ds(e, 1), :].rearrange("p a f -> p (a f)"), WS[:, u, 0:2 * F])
                nc.gpsimd.tensor_copy(W2_hi[:, bass.ds(e, 1), :].rearrange("p a f -> p (a f)"),
                                      WS[:, u, 2 * F:3 * F]).then_inc(whi_ready, 1)
                gp.wait_ge(whi_ready, e + 1)
                nc.gpsimd.tensor_tensor(W13_lo[:, bass.ds(e, 1), :].rearrange("p a f -> p (a f)"), WS[:, u, 0:2 * F],
                                        W13_hi[:, bass.ds(e, 1), :].rearrange("p a f -> p (a f)").bitcast(F32),
                                        ALU.subtract)
                nc.gpsimd.tensor_tensor(W2_lo[:, bass.ds(e, 1), :].rearrange("p a f -> p (a f)"),
                                        WS[:, u, 2 * F:3 * F],
                                        W2_hi[:, bass.ds(e, 1), :].rearrange("p a f -> p (a f)").bitcast(F32),
                                        ALU.subtract).then_inc(w_split, 1)

            def rsqrt2(t):
                gp.wait_ge(var2_ready, t + 1)
                nc.gpsimd.tensor_tensor(r2[:, :], ve2[:, :], half[:, 0:1], ALU.pow).then_inc(r2_ready, 1)

            def dispatch(t):
                gp.wait_ge(slots_ready, t + 1)
                gp.wait_ge(row_copied, t + 1)
                gp.wait_ge(weights_ready, t + 1)
                for k in range(2):
                    gp.indirect_dma_start(dispatched[:, :], bass.IndirectOffsetOnAxis(slot[:, t, k:k + 1], 0),
                                          rows[:, t, k, :], None).then_inc(rows_out, 16)

            def tile_turn(t, u, final=False):
                normalise(t, u)
                split_expert(t, u)
                rsqrt2(t - 1)

            normalise(0, 0)
            split_expert(0, 0)
            tile_turn(1, 1)
            with gp.Fori(1, TILES // 2) as i:
                for u in range(2):
                    tile_turn(2 * i + u, u)
            rsqrt2(TILES - 1)
            gp.wait_ge(regions_blank, 16)
            for t in range(TILES):
                dispatch(t)

            def send_back(s, k):
                gp.wait_ge(yo_ready, s + 1)
                gp.indirect_dma_start(returned[:, :], bass.IndirectOffsetOnAxis(RT[:, k, D:D + 1].bitcast(U32), 0),
                                      YO[:, k % 2, :], None, bounds_check=RETURN - 1,
                                      oob_is_err=False).then_inc(yo_out[k % 2], 16)

            for s in range(SLOT_TILES):
                send_back(s, s % RIN)

        @block.scalar
        def _(act):
            act.dma_start(CTX[:, :, :], ctx_in.rearrange("b j d -> j b d")).then_inc(ld_ctx, 16)
            wkv_v = wkv.rearrange("p (w d) -> p w d", w=2)
            for c in range(2):
                act.dma_start(WKV2[:, :, c, :], wkv_v).then_inc(ld_wkv, 16)
            for n, v in enumerate((ln_g, ln_b, cln_g, cln_b)):
                act.dma_start(lng[:, n:n + 1], v.rearrange(col, a=1)).then_inc(ld_vec, 16)
            for n, v in enumerate((g_xattn, g_ffn)):
                act.dma_start(gates[:, n:n + 1], v.partition_broadcast(P)).then_inc(ld_gate, 16)
            act.dma_start(GB[:, :], gate_b.partition_broadcast(P)).then_inc(ld_gw, 16)
            act.dma_start(GW[:, :], gate_w).then_inc(ld_gw, 16)

            act.wait_ge(ld_gate, 32)
            nc.scalar.activation(tg[:, :], gates[:, :], ACT.Tanh).then_inc(tg_ready, 1)
            act.wait_ge(ld_vec, 64)
            act.wait_ge(cT_ready, 1)
            nc.scalar.activation(CN[:, :], TP[1][:, 0:B * J], ACT.Identity, bias=lng[:, 3:4],
                                 scale=lng[:, 2:3]).then_inc(cn_ready, 1)
            for g in range(2):
                act.wait_ge(wqT_ready, g + 1)
                nc.scalar.activation(WQT[:, 4 * g:4 * g + 4, :].rearrange("p q d -> p (q d)"), SC[g][:, :],
                                     ACT.Copy).then_inc(wqT_used, 1)
            act.wait_ge(ld_f1, 16)
            nc.scalar.activation(F1_hi[:, :], F1[:, :], ACT.Copy).then_inc(f1hi_ready, 1)

            def affine_xn(t, u):
                act.wait_ge(xT_ready, t + 1)
                if not isinstance(t, int) or t >= 2:
                    act.wait_ge(xn_split, t - 1)
                nc.scalar.activation(XN[:, u, :], xh_T, ACT.Identity, bias=lng[:, 1:2],
                                     scale=lng[:, 0:1]).then_inc(xn_ready, 1)

            affine_xn(0, 0)
            for p in range(PAIRS):
                act.wait_ge(a_ready, p + 1)
                nc.scalar.activation(A_hi[:, :, 2 * J * p:2 * J * (p + 1)],
                                     bank[p % 5][:, 0:B * 2 * J].rearrange("p (b c) -> p b c", b=B),
                                     ACT.Copy).then_inc(ahi_ready, 1)

            def ff_tanh(t):
                act.wait_ge(gu_ready, t + 1)
                if not isinstance(t, int) or t >= 1:
                    act.wait_ge(h_ready, t)
                nc.scalar.activation(TH[:, :], GP[:, :], ACT.Tanh, scale=0.5).then_inc(tanh_ready, 1)

            def softmax_exp(t, u):
                act.wait_ge(shift_ready, t + 1)
                nc.scalar.activation(PR[:, u, :], PR[:, u, :], ACT.Exp).then_inc(exp_ready, 1)

            def copy_transposes(t, u, more):
                for q in range(4):
                    if q == 3 and more:
                        affine_xn(t + 2, 1 - u)
                    act.wait_ge(tp_ready, 4 * t + q + 1)
                    if q == 0:
                        o, i_ = HT[:, :, :].rearrange("p q d -> p (q d)"), TP[0][:, :]
                    elif q < 3:
                        o, i_ = PT[:, 4 * q - 4:4 * q, :].rearrange("p q d -> p (q d)"), TP[q % 2][:, :]
                    else:
                        nc.scalar.activation(PT[:, 8, :], TP[1][:, 0:P], ACT.Copy)
                        o, i_ = PT[0:LASTC, 9, :], TP[1][0:LASTC, P:2 * P]
                    nc.scalar.activation(o, i_, ACT.Copy).then_inc(tp_copied, 1)

            def copy_yT(t):
                act.wait_ge(yT_ready, t + 1)
                nc.scalar.activation(YT[:, :], y_T, ACT.Copy).then_inc(yT_copied, 1)

            def copy_rows(t, u):
                act.wait_ge(y_ready, t + 1)
                nc.scalar.activation(rows[:, t, :, 0:D], YB[:, u, :].unsqueeze(1).to_broadcast([P, 2, D]),
                                     ACT.Copy).then_inc(row_copied, 1)

            def gap_exp(t):
                act.wait_ge(gap_ready, t + 1)
                nc.scalar.activation(eg[:, :], gap[:, :], ACT.Exp).then_inc(eg_ready, 1)

            ff_tanh(0)
            softmax_exp(0, 0)
            for g in range(6):
                act.wait_ge(vo_ready, g + 1)
                b, c = divmod(g, 3)
                n = min(4, CH - 4 * c)
                nc.scalar.activation(VO[:, b, 4 * c:4 * c + n, :].rearrange("p q d -> p (q d)"),
                                     TP[g % 2][:, 0:n * P], ACT.Copy).then_inc(vo_used, 1)

            affine_xn(1, 1)

            def tile_turn(t, u, route=True, more=True):
                ff_tanh(t)
                if route:
                    gap_exp(t - 2)
                softmax_exp(t, u)
                copy_transposes(t - 1, u, more)
                copy_rows(t - 1, 1 - u)
                copy_yT(t - 1)

            tile_turn(1, 1, route=False)
            with act.Fori(1, TILES // 2 - 1) as i:
                for u in range(2):
                    tile_turn(2 * i + u, u)
            tile_turn(TILES - 2, 0)
            tile_turn(TILES - 1, 1, more=False)
            gap_exp(TILES - 2)
            copy_transposes(TILES - 1, 0, more=False)
            copy_rows(TILES - 1, 1)
            copy_yT(TILES - 1)
            gap_exp(TILES - 1)

            PX, GE_ps, UE_ps, HP, YP = bank[0], bank[1:3], bank[3:5], bank[5:7], bank[7]

            def slot_hi(s, u):
                act.wait_ge(sT_ready, s + 1)
                if not isinstance(s, int) or s >= 2:
                    act.wait_ge(sup_ready, s - 1)
                nc.scalar.activation(XT_hi[u][:, :], PX[:, u * P:(u + 1) * P], ACT.Copy).then_inc(shi_ready, 1)

            def silu(s, u):
                act.wait_ge(sgate_ready, s + 1)
                if not isinstance(s, int) or s >= 2:
                    act.wait_ge(he_ready, s - 1)
                nc.scalar.activation(SG[:, u, :], GE_ps[u][:, :], ACT.Silu).then_inc(silu_ready, 1)

            def ht_hi(s, u):
                act.wait_ge(heT_ready, s + 1)
                if not isinstance(s, int) or s >= 1:
                    act.wait_ge(ye_ready, s)
                nc.scalar.activation(HT_hi[:, :, :].rearrange("p q d -> p (q d)"), HP[u][:, :],
                                     ACT.Copy).then_inc(hthi_ready, 1)

            def weigh(s, k):
                act.wait_ge(ye_ready, s + 1)
                if not isinstance(s, int) or s >= 2:
                    act.wait_ge(yo_out[k % 2], s // 2 * 16)
                nc.scalar.activation(YO[:, k % 2, :], YP[:, (k % 2) * P:(k % 2 + 1) * P], ACT.Copy,
                                     scale=RT[:, k, D + 1:D + 2]).then_inc(yo_ready, 1)

            slot_hi(0, 0)
            silu(0, 0)
            slot_hi(1, 1)

            def slot_turn(s, k, u, last=0):
                ht_hi(s, u)
                if last < 2:
                    silu(s + 1, 1 - u)
                weigh(s, k)
                if last < 1:
                    slot_hi(s + 2, u)

            for s in range(3):
                slot_turn(s, s, s % 2)
            with act.Fori(0, (SLOT_TILES - 7) // 4) as i:
                for k in range(4):
                    slot_turn(4 * i + 3 + k, (3 + k) % 4, (3 + k) % 2)
            for s in range(SLOT_TILES - 4, SLOT_TILES):
                slot_turn(s, s % 4, s % 2, last=max(0, s - (SLOT_TILES - 3)))

        @block.vector
        def _(dve):
            steps = Steps(dve, dve_steps)
            nc.vector.memset(kdiag[:, :, :, :], 0.0)
            nc.vector.memset(vpad[:, :, :], 0.0).then_inc(diag_zero, 1)
            dve.wait_ge(ld_ctx, 16)
            for b in range(B):
                last = nc.vector.bn_stats(cstats[:, b, :], CTX[:, b, :])
            steps.link(last)
            for b in range(B):
                last = nc.vector.bn_aggr(cmv[:, b, :], cstats[:, b, :])
            steps.link(last)
            nc.vector.tensor_scalar(cveps[:, :], cmv[:, :, 1], EPS, None, ALU.add).then_inc(cvar_ready, 1)
            dve.wait_ge(ld_x, 16)
            for t in range(TILES):
                last = nc.vector.bn_stats(stats[:, t, :], X[:, t, :])
            steps.link(last)
            for t in range(TILES):
                last = nc.vector.bn_aggr(mv[:, t, :], stats[:, t, :])
            steps.link(last)
            nc.vector.tensor_scalar(veps[:, :], mv[:, :, 1], 1.0 + EPS, EPS * EPS, ALU.mult,
                                    ALU.add).then_inc(xvar_ready, 1)
            dve.wait_ge(crs_ready, 1)
            for b in range(B):
                nc.vector.tensor_scalar(CHAT[:, b, :], CTX[:, b, :], cmv[:, b, 0:1], rc[:, b:b + 1], ALU.subtract,
                                        ALU.mult).then_inc(chat_ready, 1)

            def xhat(t, u):
                if not isinstance(t, int) or t >= 2:
                    dve.wait_ge(xT_ready, t - 1)
                nc.vector.tensor_scalar(XH[:, u, :], X[:, t, :], mv[:, t, 0:1], rx[:, bass.ds(t, 1)], ALU.subtract,
                                        ALU.mult).then_inc(xh_ready, 1)

            def split_xn(t, u):
                dve.wait_ge(xn_ready, t + 1)
                if not isinstance(t, int) or t >= 2:
                    dve.wait_ge(gu_ready, t - 1)
                steps.link(nc.vector.tensor_copy(XN_hi[u][:, :], XN[:, u, :]))
                nc.vector.tensor_tensor(XN_lo[u][:, :], XN[:, u, :], XN_hi[u][:, :].bitcast(F32),
                                        ALU.subtract).then_inc(xn_split, 1)

            dve.wait_ge(xrs_ready, 1)
            xhat(0, 0)
            xhat(1, 1)
            dve.wait_ge(kv_ready, 1)
            kv = TP[0][:, 0:2 * B * J].rearrange("p (w b j) -> p w b j", w=2, b=B)
            for c in range(2):
                rws = slice(DH * c, DH * (c + 1))
                nc.vector.tensor_scalar(kdiag[rws, :, c, :], kv[rws, 0], DH ** -0.5, None, ALU.mult)
                last = nc.vector.tensor_copy(vpad[rws, :, P + J * c:P + J * (c + 1)], kv[rws, 1])
            last.then_inc(kv_used, 1)
            split_xn(0, 0)
            dve.wait_ge(f1hi_ready, 1)
            nc.vector.tensor_tensor(F1_lo[:, :], F1[:, :], F1_hi[:, :].bitcast(F32), ALU.subtract).then_inc(f1_split, 1)
            for p in range(PAIRS):
                dve.wait_ge(ahi_ready, p + 1)
                cs = slice(2 * J * p, 2 * J * (p + 1))
                nc.vector.tensor_tensor(A_lo[:, :, cs], bank[p % 5][:, 0:B * 2 * J].rearrange("p (b c) -> p b c", b=B),
                                        A_hi[:, :, cs].bitcast(F32), ALU.subtract).then_inc(a_used, 1)

            S4 = [SC[g][:, 0:(HB if g < 2 else TAILH) * J].rearrange("p (h j) -> p h j", j=J) for g in range(3)]
            heads = [(0, HB), (HB, 2 * HB), (2 * HB, H)]

            def read_rank(t):
                dve.wait_ge(rank_ready, t + 1)
                nc.vector.tensor_tensor(rkb[:, :], rk_ps, base_e[:, :], ALU.add).then_inc(rank_read, 1)

            def shift(t, u, route=False):
                dve.wait_ge(scores_ready, t + 1)
                for g, (a, b) in enumerate(heads):
                    last = nc.vector.tensor_reduce(M16[:, a:b], S4[g], AX_X, ALU.max)
                steps.link(last)
                if route:
                    read_rank(t - 2)
                if not isinstance(t, int) or t >= 2:
                    dve.wait_ge(tp_ready, 4 * (t - 1))
                for g, (a, b) in enumerate(heads):
                    last = nc.vector.tensor_tensor(PR[:, u, a * J:b * J].rearrange("p (h j) -> p h j", j=J), S4[g],
                                                   M16[:, a:b].unsqueeze(2).to_broadcast([P, b - a, J]), ALU.subtract)
                last.then_inc(shift_ready, 1)

            def sums(t, u):
                dve.wait_ge(exp_ready, t + 1)
                steps.link(nc.vector.tensor_reduce(RS[:, u, :], PR[:, u, :].rearrange("p (h j) -> p h j", j=J),
                                                   AX_X, ALU.add))
                nc.vector.reciprocal(RI[:, u, :], RS[:, u, :]).then_inc(rsum_ready, 1)

            def ff_h(t, u):
                dve.wait_ge(tanh_ready, t + 1)
                if not isinstance(t, int) or t >= 2:
                    dve.wait_ge(tp_ready, 4 * (t - 1) - 3)
                steps.link(nc.vector.scalar_tensor_tensor(HH[:, u, :], TH[:, :], 1.0, GP[:, :], ALU.add, ALU.mult))
                nc.vector.scalar_tensor_tensor(HH[:, u, :], HH[:, u, :], 0.5, UP[:, :], ALU.mult,
                                               ALU.mult).then_inc(h_ready, 1)

            def residual(t):
                dve.wait_ge(acc_ready, t + 1)
                steps.drained(nc.vector.scalar_tensor_tensor(X2[:, t, :], acc_ps, tg[:, 0:1], X[:, t, :], ALU.mult, ALU.add))
                steps.drained(nc.vector.bn_stats(st2[:, :], X2[:, t, :]))
                steps.link(nc.vector.bn_aggr(mv2[:, :], st2[:, :]))
                nc.vector.tensor_scalar(ve2[:, :], mv2[:, 1:2], EPS, None, ALU.add).then_inc(var2_ready, 1)

            def normed(t, u):
                dve.wait_ge(r2_ready, t + 1)
                if not isinstance(t, int) or t >= 2:
                    dve.wait_ge(row_copied, t - 1)
                    dve.wait_ge(yT_ready, t - 1)
                nc.vector.tensor_scalar(YB[:, u, :], X2[:, t, :], mv2[:, 0:1], r2[:, 0:1], ALU.subtract,
                                        ALU.mult).then_inc(y_ready, 1)

            def choose(t):
                dve.wait_ge(logits_ready, t + 1)
                steps.drained(nc.vector.tensor_tensor(LG[:, :], lg_ps, GB[:, :], ALU.add))
                steps.link(nc.vector.max(MX[:, :], LG[:, :]))
                nc.vector.tensor_tensor(gap[:, :], MX[:, 1:2], MX[:, 0:1], ALU.subtract).then_inc(gap_ready, 1)
                steps.link(nc.vector.max_index(IX[:, :], MX[:, :], LG[:, :]))
                steps.link(nc.vector.tensor_copy(IXF[:, :], IX[:, 0:2]))
                steps.link(nc.vector.tensor_tensor(pick[:, :, :], iota_e[:, :].unsqueeze(1).to_broadcast([P, 2, E]),
                                                   IXF[:, :].unsqueeze(2).to_broadcast([P, 2, E]), ALU.is_equal))
                steps.link(nc.vector.tensor_tensor(Ms[:, :], pick[:, 0, :], pick[:, 1, :], ALU.add))
                nc.vector.tensor_tensor(Macc[:, t + 1, :], Macc[:, t, :], Ms[:, :], ALU.add).then_inc(picks_ready, 1)

            def place(t):
                dve.wait_ge(eg_ready, t + 1)
                steps.link(nc.vector.tensor_scalar(wsum[:, :], eg[:, :], 1.0, None, ALU.add))
                steps.link(nc.vector.reciprocal(wone[:, :], wsum[:, :]))
                nc.vector.tensor_tensor(rows[:, t, 0, D + 1:D + 2], wone[:, :], tg[:, 1:2], ALU.mult)
                steps.link(nc.vector.tensor_tensor(wsum[:, :], wone[:, :], eg[:, :], ALU.mult))
                nc.vector.tensor_tensor(rows[:, t, 1, D + 1:D + 2], wsum[:, :], tg[:, 1:2],
                                        ALU.mult).then_inc(weights_ready, 1)
                dve.wait_ge(rank_read, t + 1)
                steps.link(nc.vector.tensor_tensor(prod[:, :, :], pick[:, :, :],
                                                   rkb[:, :].unsqueeze(1).to_broadcast([P, 2, E]), ALU.mult))
                with nc.allow_low_precision("slot numbers are whole numbers below 2^24"):
                    nc.vector.tensor_reduce(slot[:, t, :], prod[:, :, :], AX_X, ALU.add).then_inc(slots_ready, 1)

            shift(0, 0)
            ff_h(0, 0)
            sums(0, 0)
            split_xn(1, 1)
            dve.wait_ge(tg_ready, 1)
            dve.wait_ge(ld_gw, 32)
            dve.wait_ge(consts, 3)

            def tile_turn(t, u, route=True, more=True):
                shift(t, u, route)
                ff_h(t, u)
                if route:
                    place(t - 2)
                sums(t, u)
                if more:
                    xhat(t + 1, 1 - u)
                    split_xn(t + 1, 1 - u)
                residual(t - 1)
                normed(t - 1, 1 - u)
                choose(t - 1)

            TURN = 2 * 14
            shift(1, 1)
            ff_h(1, 1)
            sums(1, 1)
            xhat(2, 0)
            split_xn(2, 0)
            residual(0)
            normed(0, 0)
            choose(0)
            with dve.Fori(1, TILES // 2 - 1) as i:
                steps.enter(i, 1, TURN)
                for u in range(2):
                    tile_turn(2 * i + u, u)
            steps.leave(TILES // 2 - 2)
            tile_turn(TILES - 2, 0)
            tile_turn(TILES - 1, 1, more=False)
            read_rank(TILES - 2)
            place(TILES - 2)
            residual(TILES - 1)
            normed(TILES - 1, 1)
            choose(TILES - 1)
            read_rank(TILES - 1)
            place(TILES - 1)

            dve.wait_ge(counts_ready, 1)
            with nc.allow_low_precision("counts are whole numbers below 2^24"):
                steps.link(nc.vector.tensor_scalar(T8u[:, :], ct_ps, float(P - 1), None, ALU.add))
                steps.link(nc.vector.tensor_scalar(T8u[:, :], T8u[:, :], 7, None, ALU.logical_shift_right))
                steps.link(nc.vector.tensor_copy(Tn[:, :], T8u[:, :]))
                steps.link(nc.vector.tensor_tensor(TT[:, :, :], tri[:, :, :], Tn[:, :].unsqueeze(1).to_broadcast([1, E, E]), ALU.mult))
                steps.link(nc.vector.tensor_reduce(Tend[:, :], TT[:, :, :], AX_X, ALU.add))
                steps.link(nc.vector.tensor_tensor(GE[:, :, :], iota_s[:, :].unsqueeze(2).to_broadcast([1, SLOT_TILES, E]),
                                                   Tend[:, :].unsqueeze(1).to_broadcast([1, SLOT_TILES, E]), ALU.is_ge))
                steps.link(nc.vector.tensor_reduce(es[:, :], GE[:, :, :], AX_X, ALU.add))
                steps.link(nc.vector.tensor_tensor(GT[:, :, :], GE[:, :, :], Tn[:, :].unsqueeze(1).to_broadcast([1, SLOT_TILES, E]), ALU.mult))
                steps.link(nc.vector.tensor_reduce(ts_[:, :], GT[:, :, :], AX_X, ALU.add))
                steps.link(nc.vector.tensor_tensor(rowb[:, :], iota_s[:, :], ts_[:, :], ALU.subtract))
                steps.link(nc.vector.tensor_scalar(rowb[:, :], rowb[:, :], float(P), None, ALU.mult))
                nc.vector.tensor_scalar(expert_of[:, :], es[:, :], float(E - 1), None, ALU.min)
                nc.vector.scalar_tensor_tensor(row_of[:, :], es[:, :], float(CAP), rowb[:, :], ALU.mult,
                                               ALU.add).then_inc(tables_ready, 1)

            PX, GE_ps, UE_ps, HP = bank[0], bank[1:3], bank[3:5], bank[5:7]

            def slot_lo(s, u):
                dve.wait_ge(shi_ready, s + 1)
                nc.vector.tensor_tensor(XT_lo[u][:, :], PX[:, u * P:(u + 1) * P], XT_hi[u][:, :].bitcast(F32),
                                        ALU.subtract).then_inc(s_split, 1)

            def gate_up(s, u):
                dve.wait_ge(silu_ready, s + 1)
                dve.wait_ge(sup_ready, s + 1)
                if not isinstance(s, int) or s >= 2:
                    dve.wait_ge(heT_ready, s - 1)
                nc.vector.tensor_tensor(HE[:, u, :], SG[:, u, :], UE_ps[u][:, :], ALU.mult).then_inc(he_ready, 1)

            def ht_lo(s, u):
                dve.wait_ge(hthi_ready, s + 1)
                if not isinstance(s, int) or s >= 1:
                    dve.wait_ge(ye_ready, s)
                nc.vector.tensor_tensor(HT_lo[:, :, :].rearrange("p q d -> p (q d)"), HP[u][:, :],
                                        HT_hi[:, :, :].rearrange("p q d -> p (q d)").bitcast(F32),
                                        ALU.subtract).then_inc(ht_split, 1)

            slot_lo(0, 0)
            gate_up(0, 0)
            slot_lo(1, 1)

            def slot_turn(s, u, last=0):
                ht_lo(s, u)
                if last < 2:
                    gate_up(s + 1, 1 - u)
                if last < 1:
                    slot_lo(s + 2, u)

            slot_turn(0, 0)
            with dve.Fori(0, (SLOT_TILES - 3) // 2) as i:
                for u in (1, 0):
                    slot_turn(2 * i + 2 - u, u)
            slot_turn(SLOT_TILES - 2, 1, last=1)
            slot_turn(SLOT_TILES - 1, 0, last=2)

            dve.wait_ge(back_in, 16)
            steps.link(nc.vector.tensor_tensor(X2[:, :, :], X2[:, :, :], back[:, :, 0:D], ALU.add))
            nc.vector.tensor_tensor(X2[:, :, :], X2[:, :, :], back[:, :, D:2 * D], ALU.add).then_inc(osum_ready, 1)

        @block.tensor
        def _(pe):
            def mm3(o, l_hi, l_lo, r_hi, r_lo, start=True, stop=True):
                nc.tensor.matmul(o, l_hi, r_hi, start=start, stop=False)
                nc.tensor.matmul(o, l_lo, r_hi, start=False, stop=False)
                return nc.tensor.matmul(o, l_hi, r_lo, start=False, stop=stop)

            pe.wait_ge(consts, 2)
            pe.wait_ge(chat_ready, B)
            for b in range(B):
                last = nc.tensor.transpose(TP[1][:, b * J:(b + 1) * J], CHAT[:, b, :], identf[0:J, 0:J])
            last.then_inc(cT_ready, 1)
            pe.wait_ge(ld_wq, 16)
            for g in range(2):
                for q in range(4):
                    last = nc.tensor.transpose(SC[g][:, q * P:(q + 1) * P], WQ[:, (4 * g + q) * P:(4 * g + q + 1) * P],
                                               identf[:, :])
                last.then_inc(wqT_ready, 1)
            pe.wait_ge(ld_wkv, 32)
            pe.wait_ge(cn_ready, 1)
            for w in range(2):
                last = nc.tensor.matmul(TP[0][:, w * B * J:(w + 1) * B * J], WKV2[:, w, :, :].rearrange("p c d -> p (c d)"),
                                        CN[:, :], start=True, stop=True)
            last.then_inc(kv_ready, 1)

            def transpose_xhat(t, u):
                pe.wait_ge(xh_ready, t + 1)
                if not isinstance(t, int) or t >= 1:
                    pe.wait_ge(h_ready, t)
                nc.tensor.transpose(xh_T, XH[:, u, :], identf[:, :]).then_inc(xT_ready, 1)

            transpose_xhat(0, 0)
            pe.wait_ge(kv_used, 1)
            pe.wait_ge(wqT_used, 2)
            pe.wait_ge(xn_ready, 1)
            for p in range(PAIRS):
                if p >= 5:
                    pe.wait_ge(a_used, p - 4)
                nc.tensor.matmul(bank[p % 5][:, 0:B * 2 * J], WQT[:, p, :], kdiag[:, :, :, :].rearrange("p b c j -> p (b c j)"),
                                 start=True, stop=True).then_inc(a_ready, 1)

            def scores(t, u, b):
                pe.wait_ge(xn_split, t + 1)
                if not isinstance(t, int) or t >= 1:
                    pe.wait_ge(shift_ready, t)
                for g, (a, e) in enumerate(((0, HB), (HB, 2 * HB), (2 * HB, H))):
                    n = (e - a) * J
                    hi = A_hi[:, bass.ds(b, 1), a * J:e * J].rearrange("p a c -> p (a c)")
                    lo = A_lo[:, bass.ds(b, 1), a * J:e * J].rearrange("p a c -> p (a c)")
                    last = mm3(SC[g][:, 0:n], XN_hi[u][:, :], XN_lo[u][:, :], hi, lo)
                last.then_inc(scores_ready, 1)

            def gate_up(t, u):
                if not isinstance(t, int) or t >= 1:
                    pe.wait_ge(h_ready, t)
                for n, o in enumerate((UP, GP)):
                    cs = slice(n * FF, (n + 1) * FF)
                    last = mm3(o[:, :], XN_hi[u][:, :], XN_lo[u][:, :], F1_hi[:, cs], F1_lo[:, cs])
                last.then_inc(gu_ready, 1)

            pe.wait_ge(a_used, PAIRS)
            scores(0, 0, 0)
            pe.wait_ge(f1_split, 1)
            gate_up(0, 0)
            pe.wait_ge(ld_wo, 16)
            for g in range(6):
                b, c4 = divmod(g, 3)
                if g >= 2:
                    pe.wait_ge(vo_used, g - 1)
                for c in range(4 * c4, min(4 * c4 + 4, CH)):
                    crossed = [p for p in range(PAIRS) if 0 < P + P * c - 2 * J * p < P + 2 * J]
                    for p in crossed:
                        at = P + P * c - 2 * J * p
                        last = nc.tensor.matmul(TP[g % 2][:, (c - 4 * c4) * P:(c - 4 * c4 + 1) * P],
                                                vpad[:, b, at:at + P], WO[:, p, :],
                                                start=p == crossed[0], stop=p == crossed[-1])
                last.then_inc(vo_ready, 1)
            pe.wait_ge(vo_used, 6)
            transpose_xhat(1, 1)

            def attend(t, u, b, more=True):
                def turn(q):
                    if q == 0:
                        pe.wait_ge(h_ready, t + 1)
                        srcs = [HH[:, u, c * P:(c + 1) * P] for c in range(4)]
                    else:
                        if q == 1:
                            pe.wait_ge(probs_ready, t + 1)
                        srcs = [PR[:, u, c * P:min((c + 1) * P, HJ)] for c in range(4 * q - 4, min(4 * q, CH))]
                    if q < 2:
                        if not isinstance(t, int) or t >= 1:
                            pe.wait_ge(tp_copied, 4 * t + q - 1)
                    else:
                        pe.wait_ge(tp_copied, 4 * t + q - 1)
                    for n, s in enumerate(srcs):
                        w = s.shape[1]
                        last = nc.tensor.transpose(TP[q % 2][0:w, n * P:(n + 1) * P], s, identf[:, :])
                    last.then_inc(tp_ready, 1)

                def share(q):
                    pe.wait_ge(tp_copied, 4 * t + q + 1)
                    if q == 0:
                        if not isinstance(t, int) or t >= 1:
                            pe.wait_ge(rank_read, t)
                        for c in range(4):
                            nc.tensor.matmul(acc_ps, HT[:, c, :], F2[:, c, :], start=c == 0, stop=False)
                        return None
                    for c in range(4 * q - 4, min(4 * q, CH)):
                        k = LASTC if c == CH - 1 else P
                        last = nc.tensor.matmul(acc_ps, PT[0:k, c, :],
                                                VO[0:k, bass.ds(b, 1), c, :].rearrange("p a d -> p (a d)"),
                                                start=False, stop=c == CH - 1)
                    return last

                turn(0)
                turn(1)
                share(0)
                turn(2)
                share(1)
                if more:
                    transpose_xhat(t + 2, u)
                turn(3)
                share(2)
                share(3).then_inc(acc_ready, 1)

            def transpose_y(t, u):
                pe.wait_ge(y_ready, t + 1)
                nc.tensor.transpose(y_T, YB[:, u, :], identf[:, :]).then_inc(yT_ready, 1)

            def logits(t):
                pe.wait_ge(yT_copied, t + 1)
                nc.tensor.matmul(lg_ps, YT[:, :], GW[:, :], start=True, stop=True).then_inc(logits_ready, 1)

            def ranks(t):
                pe.wait_ge(picks_ready, t + 1)
                nc.tensor.matmul(rk_ps, lower_b[:, :], Ms[:, :], start=True, stop=False)
                nc.tensor.matmul(rk_ps, ones_b[:, :], Macc[:, bass.ds(t, 1), :].rearrange("p a e -> p (a e)"),
                                 start=False, stop=True).then_inc(rank_ready, 1)

            pe.wait_ge(ld_f2, 16)
            pe.wait_ge(ld_gw, 32)
            pe.wait_ge(consts, 3)

            def tile_turn(t, u, batch, back_batch, route=True, more=True):
                scores(t, u, batch)
                if route:
                    ranks(t - 2)
                gate_up(t, u)
                attend(t - 1, 1 - u, back_batch, more)
                transpose_y(t - 1, 1 - u)
                logits(t - 1)

            tile_turn(1, 1, 0, 0, route=False)
            with pe.Fori(1, TILES // 2 - 1) as i:
                for u in range(2):
                    t = 2 * i + u
                    tile_turn(t, u, t // PER_BATCH, (t - 1) // PER_BATCH)
            tile_turn(TILES - 2, 0, B - 1, B - 1)
            tile_turn(TILES - 1, 1, B - 1, B - 1, more=False)
            ranks(TILES - 2)
            attend(TILES - 1, 1, B - 1, more=False)
            transpose_y(TILES - 1, 1)
            logits(TILES - 1)
            ranks(TILES - 1)
            pe.wait_ge(rank_read, TILES)
            nc.tensor.matmul(ct_ps, ones_b[:, 0:1], Macc[:, TILES, :], start=True, stop=True).then_inc(counts_ready, 1)

            PX, GE_ps, UE_ps, HP, YP = bank[0], bank[1:3], bank[3:5], bank[5:7], bank[7]
            pe.wait_ge(tables_ready, 1)
            pe.wait_ge(w_split, E)

            def transpose_slots(s, k, u):
                pe.wait_ge(rt_in[k], (s // 4 + 1) * 16)
                if not isinstance(s, int) or s >= 1:
                    pe.wait_ge(s_split, s)
                nc.tensor.transpose(PX[:, u * P:(u + 1) * P], RT[:, k, 0:D], identf[:, :]).then_inc(sT_ready, 1)

            def slot_expert(s):
                return pe.value_load(expert_of[0:1, bass.ds(s, 1)], min_val=0, max_val=E - 1)

            def slot_gate_up(s, u, e):
                pe.wait_ge(s_split, s + 1)
                if not isinstance(s, int) or s >= 2:
                    pe.wait_ge(he_ready, s - 1)
                for n, (o, done) in enumerate(((GE_ps, sgate_ready), (UE_ps, sup_ready))):
                    cs = slice(n * F, (n + 1) * F)
                    mm3(o[u][:, :], XT_hi[u][:, :], XT_lo[u][:, :],
                        W13_hi[:, bass.ds(e, 1), cs].rearrange("p a f -> p (a f)"),
                        W13_lo[:, bass.ds(e, 1), cs].rearrange("p a f -> p (a f)")).then_inc(done, 1)

            def transpose_h(s, u):
                pe.wait_ge(he_ready, s + 1)
                if not isinstance(s, int) or s >= 2:
                    pe.wait_ge(ht_split, s - 1)
                for c in range(FC):
                    last = nc.tensor.transpose(HP[u][:, c * P:(c + 1) * P], HE[:, u, c * P:(c + 1) * P], identf[:, :])
                last.then_inc(heT_ready, 1)

            def slot_down(s, u, e):
                pe.wait_ge(ht_split, s + 1)
                if not isinstance(s, int) or s >= 1:
                    pe.wait_ge(yo_ready, s)
                for c in range(FC):
                    cs = slice(c * P, (c + 1) * P)
                    last = mm3(YP[:, u * P:(u + 1) * P], HT_hi[:, c, :], HT_lo[:, c, :],
                               W2_hi[:, bass.ds(e, 1), cs].rearrange("p a f -> p (a f)"),
                               W2_lo[:, bass.ds(e, 1), cs].rearrange("p a f -> p (a f)"),
                               start=c == 0, stop=c == FC - 1)
                last.then_inc(ye_ready, 1)

            transpose_slots(0, 0, 0)
            slot_gate_up(0, 0, slot_expert(0))
            transpose_slots(1, 1, 1)

            def slot_turn(s, k, u, last=0):
                transpose_h(s, u)
                if last < 2:
                    slot_gate_up(s + 1, 1 - u, slot_expert(s + 1))
                slot_down(s, u, slot_expert(s))
                if last < 1:
                    transpose_slots(s + 2, (k + 2) % 4, u)

            for s in range(3):
                slot_turn(s, s, s % 2)
            with pe.Fori(0, (SLOT_TILES - 7) // 4) as i:
                for k in range(4):
                    slot_turn(4 * i + 3 + k, (3 + k) % 4, (3 + k) % 2)
            for s in range(SLOT_TILES - 4, SLOT_TILES):
                slot_turn(s, s % 4, s % 2, last=max(0, s - (SLOT_TILES - 3)))


_INS = ['x', 'ctx_1024', 'g_xattn', 'g_ffn', 'L0_xattn_ln_g', 'L0_xattn_ln_b', 'L0_xattn_cln_g', 'L0_xattn_cln_b',
        'L0_xattn_Wq', 'L0_xattn_Wkv', 'L0_xattn_Wo', 'L0_xattn_Wff1', 'L0_xattn_Wff2', 'L0_ffn_gate_w',
        'L0_ffn_gate_b', 'L0_ffn_w1', 'L0_ffn_w3', 'L0_ffn_w2']
_OUTS = [((2, 512, 128), 'float32')]


def kernel(**inputs):
    import numpy as _np
    import concourse.bacc as _bacc
    from concourse import mybir as _mybir
    from concourse.bass_utils import run_bass_kernel_spmd as _run

    nc = _bacc.Bacc("TRN2", target_bir_lowering=False, num_devices=1)
    arrays, args = {}, []
    for name in _INS:
        a = _np.ascontiguousarray(inputs[name])
        arrays[f"in_{name}_dram"] = a
        args.append(nc.dram_tensor(f"in_{name}_dram", a.shape, _mybir.dt.from_np(a.dtype), kind="ExternalInput").ap())
    for i, (shape, dtype) in enumerate(_OUTS):
        dt = _mybir.dt.from_np(_np.dtype(dtype))
        args.append(nc.dram_tensor(f"out_{i}_dram", shape, dt, kind="ExternalOutput").ap())
    gated_block_kernel(nc, *args)
    r = _run(nc, [arrays], core_ids=[0])
    return r.results[0]["out_0_dram"]
```

```python
from contextlib import ExitStack

import concourse.bass as bass
from concourse import mybir

ALU = mybir.AluOpType
ACT = mybir.ActivationFunctionType
AX_X = mybir.AxisListType.X
F32 = mybir.dt.float32
F32R = mybir.dt.float32r
BF16 = mybir.dt.bfloat16
U32 = mybir.dt.uint32
I32 = mybir.dt.int32
P = 128


class Steps:

    def __init__(self, engine, semaphore):
        self.engine, self.semaphore, self.count, self.shift = engine, semaphore, 0, 0

    def link(self, instruction):
        self.did(instruction)
        self.wait()

    def did(self, instruction):
        instruction.then_inc(self.semaphore, 1)
        self.count += 1

    def wait(self):
        self.engine.wait_ge(self.semaphore, self.count + self.shift)

    def enter(self, turn, first, per_turn):
        self.begin, self.per_turn = self.count, per_turn
        self.shift = (turn - first) * per_turn

    def leave(self, turns):
        assert self.count - self.begin == self.per_turn, (self.count - self.begin, self.per_turn)
        self.count, self.shift = self.begin + turns * self.per_turn, 0


def gated_block_kernel(nc, x, ctx_in, g_xattn, g_ffn, ln_g, ln_b, cln_g, cln_b, wq, wkv, wo, wff1, wff2,
                       gate_w, gate_b, w1, w3, w2, out):
    B, N, D = x.shape
    J = ctx_in.shape[1]
    INNER = wq.shape[1]
    DH = wkv.shape[1] // 2
    H = INNER // DH
    FF = wff2.shape[0]
    E, _, F = w1.shape
    EPS = 1e-5
    TILES = B * N // P
    PER_BATCH = N // P
    HJ = H * J
    PAIRS = H // 2
    CH = -(-HJ // P)
    LASTC = HJ - (CH - 1) * P
    HB = 6
    TAILH = H - 2 * HB
    FC = F // P
    CAP = TILES * P
    SLOT_TILES = (2 * B * N - E) // P + E
    SPARE = SLOT_TILES - 2 * B * N // P
    REGION = E * CAP + SPARE * P
    ROW = D + 2
    RETURN = 2 * B * N
    assert D == P and 2 * DH == P and F == 4 * P and FF == 4 * P and HB * J <= 512 and TILES % 2 == 0

    dispatched = nc.dram_tensor("dispatched", (REGION, ROW), F32, kind="Internal").ap()
    returned = nc.dram_tensor("returned", (RETURN, D), F32, kind="Internal").ap()

    with ExitStack() as ctx:
        def sb(name, shape, dt=F32):
            return ctx.enter_context(nc.sbuf_tensor(name, shape, dt))

        def sem(name):
            return ctx.enter_context(nc.semaphore(name))

        X = sb("X", [P, TILES, D])
        X2 = sb("X2", [P, TILES, D])
        CTX = sb("CTX", [J, B, D])
        CHAT = sb("CHAT", [J, B, D])
        CN = sb("CN", [P, B * J])
        WKV2 = sb("WKV2", [P, 2, 2, DH])
        kdiag = sb("kdiag", [P, B, 2, J])
        VP = P + 2 * J + P
        vpad = sb("vpad", [P, B, VP])
        early = sb("early", [P, 2 * INNER])
        WQ = early[:, 0:INNER]
        WQT = early[:, INNER:2 * INNER].rearrange("p (q d) -> p q d", d=D)
        PT = early[:, 0:CH * P].rearrange("p (q d) -> p q d", d=P)
        PR = sb("PR", [P, 2, HJ])
        F1 = PR[:, 0, 0:2 * FF]
        WO = PR[:, 1, 0:INNER].rearrange("p (q d) -> p q d", d=D)
        back = PR[:, :, :].rearrange("p u c -> p (u c)")[:, 0:TILES * 2 * D].rearrange("p (t c) -> p t c", c=2 * D)
        A_hi = sb("A_hi", [P, B, HJ], F32R)
        A_lo = sb("A_lo", [P, B, HJ], F32R)
        VO = sb("VO", [P, B, CH, D])
        F1_hi = sb("F1_hi", [P, 2 * FF], F32R)
        F1_lo = sb("F1_lo", [P, 2 * FF], F32R)
        F2 = sb("F2", [P, FF // P, D])
        lng = sb("lng", [P, 4])
        gates = sb("gates", [P, 2])
        tg = sb("tg", [P, 2])
        GW = sb("GW", [P, E])
        GB = sb("GB", [P, E])
        half = sb("half", [P, TILES])
        stats = sb("stats", [P, TILES, 6])
        mv = sb("mv", [P, TILES, 2])
        veps = sb("veps", [P, TILES])
        rx = sb("rx", [P, TILES])
        cstats = sb("cstats", [J, B, 6])
        cmv = sb("cmv", [J, B, 2])
        cveps = sb("cveps", [J, B])
        rc = sb("rc", [J, B])
        identf = sb("identf", [P, P])
        ones_b = sb("ones_b", [P, P], BF16)
        lower_b = sb("lower_b", [P, P], BF16)
        iota_e = sb("iota_e", [P, E])
        base_e = sb("base_e", [P, E])
        dest0 = sb("dest0", [P, 2, 2], U32)
        pair_step = sb("pair_step", [P, 2, 2], U32)
        padrow = sb("padrow", [P, ROW])
        XH = sb("XH", [P, 2, D])
        XN = sb("XN", [P, 2, P])
        xnT_hi = sb("xnT_hi", [P, TILES, P], F32R)
        xnT_lo = sb("xnT_lo", [P, TILES, P], F32R)
        XN_hi = [sb(f"XN_hi{u}", [P, P], F32R) for u in range(2)]
        XN_lo = [sb(f"XN_lo{u}", [P, P], F32R) for u in range(2)]
        nM = sb("nM", [P, 2, H])
        RS = sb("RS", [P, 2, H])
        RI = sb("RI", [P, 2, H])
        SG = sb("SG", [P, 2, F])
        HH = sb("HH", [P, 2, F])
        HT = sb("HT", [P, 2, FC, P])
        st2 = sb("st2", [P, 2, 6])
        mv2 = sb("mv2", [P, 2, 2])
        ve2 = sb("ve2", [P, 2])
        r2 = sb("r2", [P, 2])
        YB = sb("YB", [P, 2, D])
        YT = sb("YT", [P, 2, P])
        rows = sb("rows", [P, 2, 2, ROW])
        LG = sb("LG", [P, 2, E])
        MX = sb("MX", [P, 2, 8])
        IX = sb("IX", [P, 2, 8], U32)
        IXF = sb("IXF", [P, 2, 2])
        ntop = sb("ntop", [P, 2])
        e2 = sb("e2", [P, 2, 2])
        esum = sb("esum", [P, 2])
        esinv = sb("esinv", [P, 2])
        pick = sb("pick", [P, 2, 2, E])
        Ms = sb("Ms", [P, 2, E], BF16)
        Macc = sb("Macc", [P, TILES + 1, E], BF16)
        rkb = sb("rkb", [P, 2, E])
        prod = sb("prod", [P, 2, 2, E])
        slot = sb("slot", [P, 2, 2], U32)
        T8u = sb("T8u", [1, E], U32)
        Tn = sb("Tn", [1, E])
        tri = sb("tri", [1, E, E])
        TT = sb("TT", [1, E, E])
        Tend = sb("Tend", [1, E])
        iota_s = sb("iota_s", [1, SLOT_TILES])
        GE = sb("GE", [1, SLOT_TILES, E])
        GT = sb("GT", [1, SLOT_TILES, E])
        es = sb("es", [1, SLOT_TILES])
        ts_ = sb("ts_", [1, SLOT_TILES])
        rowb = sb("rowb", [1, SLOT_TILES])
        expert_of = sb("expert_of", [1, SLOT_TILES], I32)
        row_of = sb("row_of", [1, SLOT_TILES], I32)
        WS = sb("WS", [P, 2, 2 * F])
        W13_hi = sb("W13_hi", [P, E, 2 * F], F32R)
        W13_lo = sb("W13_lo", [P, E, 2 * F], F32R)
        W2 = sb("W2", [P, E, F])
        RIN = 6
        RT = WS[:, 0, 0:RIN * ROW].rearrange("p (k c) -> p k c", c=ROW)
        YO = WS[:, 1, 0:RIN * D].rearrange("p (k c) -> p k c", c=D)
        XT_hi, XT_lo = XN_hi, XN_lo

        bank = [ctx.enter_context(nc.psum_tensor(f"bank{i}", [P, 512], F32)) for i in range(8)]
        GP, UP, HP, XP, DP = bank[0:2], bank[2:4], bank[4:6], bank[6], bank[7]
        SC, TP, AP, YP, RP = bank[0:3], bank[3:5], bank[5], bank[6], bank[7]
        acc_ps = AP[:, 0:2 * D].rearrange("p (u d) -> p u d", d=D)
        y_T = YP[:, 0:2 * P].rearrange("p (u d) -> p u d", d=P)
        lg_ps = YP[:, 256:256 + 2 * E].rearrange("p (u e) -> p u e", e=E)
        rk_ps = RP[:, 0:2 * E].rearrange("p (u e) -> p u e", e=E)
        ct_ps = RP[0:1, 64:64 + E]

        ld_ctx, ld_x, ld_wkv, ld_vec, ld_gate = sem("ld_ctx"), sem("ld_x"), sem("ld_wkv"), sem("ld_vec"), sem("ld_gate")
        ld_wq, ld_wo, ld_f1, ld_f2, ld_gw = sem("ld_wq"), sem("ld_wo"), sem("ld_f1"), sem("ld_f2"), sem("ld_gw")
        ld_ws = [sem(f"ld_ws{u}") for u in range(2)]
        ld_w2 = sem("ld_w2")
        regions_blank = sem("regions_blank")
        consts = sem("consts")
        cvar_ready, crs_ready, chat_ready = sem("cvar_ready"), sem("crs_ready"), sem("chat_ready")
        xvar_ready, xrs_ready = sem("xvar_ready"), sem("xrs_ready")
        cT_ready, cn_ready, kv_ready, kv_used = sem("cT_ready"), sem("cn_ready"), sem("kv_ready"), sem("kv_used")
        wqT_ready, wqT_used = sem("wqT_ready"), sem("wqT_used")
        a_ready, ahi_ready, a_used = sem("a_ready"), sem("ahi_ready"), sem("a_used")
        vo_ready, vo_used = sem("vo_ready"), sem("vo_used")
        f1hi_ready, f1_split = sem("f1hi_ready"), sem("f1_split")
        tg_ready = sem("tg_ready")
        xh_ready, xT_ready, xn_ready, xn_split, xn_kept = (
            sem("xh_ready"), sem("xT_ready"), sem("xn_ready"), sem("xn_split"), sem("xn_kept"))
        fg_ready, fu_ready, fsilu_ready, fh_ready = sem("fg_ready"), sem("fu_ready"), sem("fsilu_ready"), sem("fh_ready")
        fhT_ready, fhT_copied, ff_ready, ff_added = sem("fhT_ready"), sem("fhT_copied"), sem("ff_ready"), sem("ff_added")
        whi_ready, w_split = sem("whi_ready"), sem("w_split")
        xn_held = sem("xn_held")
        scores_ready, nmax_ready, shift_ready, exp_ready = (
            sem("scores_ready"), sem("nmax_ready"), sem("shift_ready"), sem("exp_ready"))
        rsum_ready, probs_ready = sem("rsum_ready"), sem("probs_ready")
        tp_ready, tp_copied, acc_ready = sem("tp_ready"), sem("tp_copied"), sem("acc_ready")
        var2_ready, r2_ready, y_ready = sem("var2_ready"), sem("r2_ready"), sem("y_ready")
        yT_ready, yT_copied, row_copied = sem("yT_ready"), sem("yT_copied"), sem("row_copied")
        acc_read, rank_read = sem("acc_read"), sem("rank_read")
        logits_ready, ntop_ready, e2_ready = sem("logits_ready"), sem("ntop_ready"), sem("e2_ready")
        picks_ready, rank_ready, slots_ready = sem("picks_ready"), sem("rank_ready"), sem("slots_ready")
        rows_out = sem("rows_out")
        counts_ready, tables_ready = sem("counts_ready"), sem("tables_ready")
        rt_in = [sem(f"rt_in{k}") for k in range(RIN)]
        sT_ready, shi_ready, s_split = sem("sT_ready"), sem("shi_ready"), sem("s_split")
        sgate_ready, sup_ready, silu_ready, he_ready = sem("sgate_ready"), sem("sup_ready"), sem("silu_ready"), sem("he_ready")
        heT_ready, heT_copied = sem("heT_ready"), sem("heT_copied")
        ye_ready, yo_ready = sem("ye_ready"), sem("yo_ready")
        yo_out = [sem(f"yo_out{k}") for k in range(RIN)]
        back_in, osum_ready, out_done = sem("back_in"), sem("osum_ready"), sem("out_done")
        dve_steps = sem("dve_steps")
        pool_steps = sem("pool_steps")

        x_v = x.rearrange("b (t p) d -> p (b t) d", p=P)
        out_v = out.rearrange("b (t p) d -> p (b t) d", p=P)
        PAIR_TURNS = TILES // 2

        def from_(t, k):
            return not isinstance(t, int) or t >= k

        def ahead(t, k):
            return not isinstance(t, int) or t + k < TILES

        def slots_ahead(s, k):
            return not isinstance(s, int) or s + k < SLOT_TILES

        def tile_loop(engine, turn):
            turn(0, 0)
            turn(1, 1)
            with engine.Fori(1, PAIR_TURNS - 1) as i:
                for u in range(2):
                    turn(2 * i + u, u)
            turn(TILES - 2, 0)
            turn(TILES - 1, 1)

        def slot_loop(engine, turn):
            for s in range(RIN):
                turn(s, s, s % 2)
            with engine.Fori(1, (SLOT_TILES - 2) // RIN) as i:
                for k in range(RIN):
                    turn(RIN * i + k, k, k % 2)
            for s in range((SLOT_TILES - 2) // RIN * RIN, SLOT_TILES):
                turn(s, s % RIN, s % 2)

        block = ctx.enter_context(nc.Block())

        @block.sync
        def _(sp):
            sp.dma_start(X[:, :, :], x_v).then_inc(ld_x, 16)
            sp.dma_start(F1, wff1).then_inc(ld_f1, 16)
            sp.dma_start(F2[:, :, :], wff2.rearrange("(q p) d -> p q d", p=P)).then_inc(ld_f2, 16)

            def load_expert(e, u):
                if from_(e, 2):
                    sp.wait_ge(w_split, e - 1)
                sp.dma_start(WS[:, u, 0:F], w1[bass.ds(e, 1)].rearrange("a d f -> d (a f)")).then_inc(ld_ws[u], 16)
                sp.dma_start(WS[:, u, F:2 * F], w3[bass.ds(e, 1)].rearrange("a d f -> d (a f)")).then_inc(ld_ws[u], 16)

            load_expert(0, 0)
            load_expert(1, 1)
            sp.dma_start(WQ, wq).then_inc(ld_wq, 16)
            sp.dma_start(WO, wo.rearrange("(q p) d -> p q d", p=P)).then_inc(ld_wo, 16)
            sp.wait_ge(consts, 1)
            half_r = REGION // P // 2 * P
            for r0, r1 in ((0, half_r), (half_r, REGION)):
                sp.dma_start(dispatched[r0:r1].rearrange("(t p) c -> p t c", p=P),
                             padrow[:, :].unsqueeze(1).to_broadcast([P, (r1 - r0) // P, ROW])).then_inc(regions_blank, 16)
            with sp.Fori(1, E // 2) as i:
                for u in range(2):
                    load_expert(2 * i + u, u)
            for e in range(E):
                sp.dma_start(W2[:, e, :].rearrange("p (q d) -> p q d", d=D),
                             w2[e].rearrange("(q p) d -> p q d", p=P)).then_inc(ld_w2, 16)

            sp.wait_ge(w_split, E)
            sp.wait_ge(tables_ready, 1)
            sp.wait_ge(rows_out, 2 * TILES * 16)

            def load_slots(s, k):
                if from_(s, RIN):
                    sp.wait_ge(yo_out[k], (s // RIN) * 16)
                row = sp.value_load(row_of[0:1, bass.ds(s, 1)], min_val=0, max_val=REGION - P)
                sp.dma_start(RT[:, k, :], dispatched[bass.ds(row, P), :]).then_inc(rt_in[k], 16)

            slot_loop(sp, lambda s, k, u: load_slots(s, k))

            for k in range(RIN):
                sp.wait_ge(yo_out[k], len(range(k, SLOT_TILES, RIN)) * 16)
            sp.dma_start(back, returned.rearrange("(t p k) d -> p t (k d)", p=P, k=2)).then_inc(back_in, 16)
            sp.wait_ge(osum_ready, 1)
            sp.dma_start(out_v, X2[:, :, :]).then_inc(out_done, 16)
            sp.wait_ge(out_done, 16)

        @block.gpsimd
        def _(gp):
            steps = Steps(gp, pool_steps)
            nc.gpsimd.memset(padrow[:, 0:D], 0.0)
            nc.gpsimd.memset(padrow[:, D + 1:ROW], 0.0)
            steps.link(nc.gpsimd.iota(padrow[:, D:D + 1].bitcast(U32), pattern=[[0, 1]], base=RETURN, channel_multiplier=0))
            nc.gpsimd.memset(half[:, :], -0.5).then_inc(consts, 1)
            steps.link(nc.gpsimd.memset(identf[:, :], 0.0))
            nc.gpsimd.affine_select(out=identf[:, :], in_=identf[:, :], compare_op=ALU.not_equal, fill=1.0,
                                    base=0, pattern=[[-1, P]], channel_multiplier=1).then_inc(consts, 1)
            gp.wait_ge(cvar_ready, 1)
            nc.gpsimd.tensor_tensor(rc[:, :], cveps[:, :], half[0:J, 0:B], ALU.pow).then_inc(crs_ready, 1)
            gp.wait_ge(xvar_ready, 1)
            nc.gpsimd.tensor_tensor(rx[:, :], veps[:, :], half[:, :], ALU.pow).then_inc(xrs_ready, 1)
            steps.link(nc.gpsimd.memset(ones_b[:, :], 1.0))
            nc.gpsimd.affine_select(out=lower_b[:, :], in_=ones_b[:, :], compare_op=ALU.is_gt, fill=0.0,
                                    base=0, pattern=[[1, P]], channel_multiplier=-1)
            nc.gpsimd.iota(iota_e[:, :], pattern=[[1, E]], base=0, channel_multiplier=0,
                           allow_small_or_imprecise_dtypes=True)
            nc.gpsimd.iota(base_e[:, :], pattern=[[CAP, E]], base=0, channel_multiplier=0,
                           allow_small_or_imprecise_dtypes=True)
            nc.gpsimd.iota(iota_s[:, :], pattern=[[1, SLOT_TILES]], base=0, channel_multiplier=0,
                           allow_small_or_imprecise_dtypes=True)
            nc.gpsimd.iota(dest0[:, :, :], pattern=[[2 * P, 2], [1, 2]], base=0, channel_multiplier=2)
            nc.gpsimd.iota(pair_step[:, :, :], pattern=[[0, 2], [0, 2]], base=4 * P, channel_multiplier=0)
            steps.link(nc.gpsimd.memset(tri[:, :, :], 1.0))
            steps.link(nc.gpsimd.affine_select(out=tri[:, :, :], in_=tri[:, :, :], compare_op=ALU.is_ge, fill=0.0,
                                               base=0, pattern=[[1, E], [-1, E]], channel_multiplier=0))
            steps.link(nc.gpsimd.memset(Macc[:, 0, :], 0.0))
            row_dest = rows[:, :, :, D:D + 1].bitcast(U32).rearrange("p t k a -> p t (k a)")
            nc.gpsimd.tensor_copy(row_dest, dest0[:, :, :]).then_inc(consts, 1)

            def expert_lo(e, u):
                gp.wait_ge(whi_ready, e + 1)
                nc.gpsimd.tensor_tensor(W13_lo[:, bass.ds(e, 1), :].rearrange("p a f -> p (a f)"), WS[:, u, :],
                                        W13_hi[:, bass.ds(e, 1), :].rearrange("p a f -> p (a f)").bitcast(F32),
                                        ALU.subtract).then_inc(w_split, 1)

            tile_loop(gp, expert_lo)

            def normalise(t, u):
                gp.wait_ge(rsum_ready, t + 1)
                v = PR[:, u, :].rearrange("p (h j) -> p h j", j=J)
                nc.gpsimd.tensor_tensor(v, v, RI[:, u, :].unsqueeze(2).to_broadcast([P, H, J]),
                                        ALU.mult).then_inc(probs_ready, 1)

            def rsqrt2(i):
                gp.wait_ge(var2_ready, i + 1)
                nc.gpsimd.tensor_tensor(r2[:, :], ve2[:, :], half[:, 0:2], ALU.pow).then_inc(r2_ready, 1)

            def dispatch(i):
                gp.wait_ge(slots_ready, i + 1)
                gp.wait_ge(row_copied, i + 1)
                if from_(i, 1):
                    gp.wait_ge(rows_out, i * 64)
                    nc.gpsimd.tensor_tensor(row_dest, row_dest, pair_step[:, :, :], ALU.add)
                gp.drain()
                gp.wait_ge(regions_blank, 32)
                for n in range(2):
                    for k in range(2):
                        gp.indirect_dma_start(dispatched[:, :], bass.IndirectOffsetOnAxis(slot[:, n, k:k + 1], 0),
                                              rows[:, n, k, :], None).then_inc(rows_out, 16)

            def pair_turn(i):
                normalise(2 * i, 0)
                if from_(i, 1):
                    rsqrt2(i - 1)
                normalise(2 * i + 1, 1)
                if from_(i, 1):
                    dispatch(i - 1)

            pair_turn(0)
            pair_turn(1)
            with gp.Fori(2, PAIR_TURNS) as i:
                pair_turn(i)
            rsqrt2(PAIR_TURNS - 1)
            dispatch(PAIR_TURNS - 1)

            for s in range(SLOT_TILES):
                k = s % RIN
                gp.wait_ge(yo_ready, s + 1)
                gp.indirect_dma_start(returned[:, :], bass.IndirectOffsetOnAxis(RT[:, k, D:D + 1].bitcast(U32), 0),
                                      YO[:, k, :], None, bounds_check=RETURN - 1,
                                      oob_is_err=False).then_inc(yo_out[k], 16)

        @block.scalar
        def _(act):
            for n, v in enumerate((ln_g, ln_b, cln_g, cln_b)):
                act.dma_start(lng[:, n:n + 1], v.rearrange("(p a) -> p a", a=1)).then_inc(ld_vec, 16)
            act.dma_start(CTX[:, :, :], ctx_in.rearrange("b j d -> j b d")).then_inc(ld_ctx, 16)
            for n, v in enumerate((g_xattn, g_ffn)):
                act.dma_start(gates[:, n:n + 1], v.partition_broadcast(P)).then_inc(ld_gate, 16)
            wkv_v = wkv.rearrange("p (w d) -> p w d", w=2)
            for c in range(2):
                act.dma_start(WKV2[:, :, c, :], wkv_v).then_inc(ld_wkv, 16)
            act.dma_start(GB[:, :], gate_b.partition_broadcast(P)).then_inc(ld_gw, 16)
            act.dma_start(GW[:, :], gate_w).then_inc(ld_gw, 16)

            act.wait_ge(ld_gate, 32)
            nc.scalar.activation(tg[:, :], gates[:, :], ACT.Tanh).then_inc(tg_ready, 1)
            act.wait_ge(ld_f1, 16)
            nc.scalar.activation(F1_hi[:, :], F1, ACT.Copy).then_inc(f1hi_ready, 1)
            act.wait_ge(ld_vec, 64)

            def affine_xn(t, u):
                act.wait_ge(xT_ready, t + 1)
                if from_(t, 2):
                    act.wait_ge(xn_split, t - 1)
                nc.scalar.activation(XN[:, u, :], XP[:, 0:P], ACT.Identity, bias=lng[:, 1:2],
                                     scale=lng[:, 0:1]).then_inc(xn_ready, 1)

            affine_xn(0, 0)
            affine_xn(1, 1)

            def keep_xn(t, u):
                act.wait_ge(xn_split, t + 1)
                nc.scalar.activation(xnT_hi[:, t, :], XN_hi[u][:, :].bitcast(F32), ACT.Copy)
                nc.scalar.activation(xnT_lo[:, t, :], XN_lo[u][:, :].bitcast(F32), ACT.Copy).then_inc(xn_kept, 1)

            def copy_hT(t, u):
                act.wait_ge(fhT_ready, t + 1)
                if from_(t, 2):
                    act.wait_ge(ff_ready, t - 1)
                nc.scalar.activation(HT[:, u, :, :].rearrange("p q d -> p (q d)"), HP[u][:, :],
                                     ACT.Copy).then_inc(fhT_copied, 1)

            def ff_turn(t, u):
                if from_(t, 1):
                    copy_hT(t - 1, 1 - u)
                act.wait_ge(fg_ready, t + 1)
                if from_(t, 2):
                    act.wait_ge(fh_ready, t - 1)
                nc.scalar.activation(SG[:, u, :], GP[u][:, :], ACT.Silu).then_inc(fsilu_ready, 1)
                keep_xn(t, u)
                if ahead(t, 2):
                    affine_xn(t + 2, u)
                act.wait_ge(ld_ws[u], (t // 2 + 1) * 32)
                nc.scalar.activation(W13_hi[:, t, :], WS[:, u, :], ACT.Copy).then_inc(whi_ready, 1)

            tile_loop(act, ff_turn)
            copy_hT(TILES - 1, 1)

            act.wait_ge(cT_ready, 1)
            nc.scalar.activation(CN[:, :], XP[:, 0:B * J], ACT.Identity, bias=lng[:, 3:4],
                                 scale=lng[:, 2:3]).then_inc(cn_ready, 1)
            for g in range(2):
                act.wait_ge(wqT_ready, g + 1)
                nc.scalar.activation(WQT[:, 4 * g:4 * g + 4, :].rearrange("p q d -> p (q d)"), GP[g][:, :],
                                     ACT.Copy).then_inc(wqT_used, 1)
            for p in range(PAIRS):
                act.wait_ge(a_ready, p + 1)
                nc.scalar.activation(A_hi[:, :, 2 * J * p:2 * J * (p + 1)],
                                     bank[p % 5][:, 0:B * 2 * J].rearrange("p (b c) -> p b c", b=B),
                                     ACT.Copy).then_inc(ahi_ready, 1)

            def hold_xn(t, u):
                if from_(t, 2):
                    act.wait_ge(scores_ready, t - 1)
                nc.scalar.activation(XN_hi[u][:, :], xnT_hi[:, t, :].bitcast(F32), ACT.Copy)
                nc.scalar.activation(XN_lo[u][:, :], xnT_lo[:, t, :].bitcast(F32), ACT.Copy).then_inc(xn_held, 1)

            def softmax_exp(t, u):
                act.wait_ge(nmax_ready, t + 1)
                if from_(t, 2):
                    act.wait_ge(tp_ready, 3 * (t - 1))
                for h in range(2 * HB, H):
                    nc.scalar.activation(PR[:, u, h * J:(h + 1) * J], SC[2][:, (h - 2 * HB) * J:(h - 2 * HB + 1) * J],
                                         ACT.Exp, bias=nM[:, u, h:h + 1])
                act.wait_ge(shift_ready, t + 1)
                v = PR[:, u, 0:2 * HB * J]
                nc.scalar.activation(v, v, ACT.Exp).then_inc(exp_ready, 1)

            def copy_probs(t):
                for q in range(3):
                    act.wait_ge(tp_ready, 3 * t + q + 1)
                    if from_(t, 1):
                        act.wait_ge(acc_ready, t)
                    if q < 2:
                        o, i_ = PT[:, 4 * q:4 * q + 4, :].rearrange("p q d -> p (q d)"), TP[q % 2][:, :]
                    else:
                        tp = TP[q % 2]
                        nc.scalar.activation(PT[:, 8, :], tp[:, 0:P], ACT.Copy)
                        o, i_ = PT[0:LASTC, 9, :], tp[0:LASTC, P:2 * P]
                    nc.scalar.activation(o, i_, ACT.Copy).then_inc(tp_copied, 1)

            def pass_rows(i):
                act.wait_ge(yT_ready, i + 1)
                nc.scalar.activation(YT[:, :, :], y_T, ACT.Copy).then_inc(yT_copied, 1)
                if from_(i, 1):
                    act.wait_ge(rows_out, i * 64)
                for k in range(2):
                    last = nc.scalar.activation(rows[:, :, k, 0:D], YB[:, :, :], ACT.Copy)
                last.then_inc(row_copied, 1)

            def weigh_choices(i):
                act.wait_ge(ntop_ready, i + 1)
                if from_(i, 1):
                    act.wait_ge(slots_ready, i)
                for n in range(2):
                    last = nc.scalar.activation(e2[:, n, :], MX[:, n, 0:2], ACT.Exp, bias=ntop[:, n:n + 1],
                                                accum_out=esum[:, n:n + 1])
                last.then_inc(e2_ready, 1)

            def pair_turn(i):
                hold_xn(2 * i, 0)
                hold_xn(2 * i + 1, 1)
                softmax_exp(2 * i, 0)
                if from_(i, 1):
                    copy_probs(2 * i - 1)
                softmax_exp(2 * i + 1, 1)
                if from_(i, 1):
                    pass_rows(i - 1)
                copy_probs(2 * i)
                if from_(i, 1):
                    weigh_choices(i - 1)

            hold_xn(0, 0)
            hold_xn(1, 1)
            softmax_exp(0, 0)
            for g in range(6):
                act.wait_ge(vo_ready, g + 1)
                b, c = divmod(g, 3)
                n = min(4, CH - 4 * c)
                nc.scalar.activation(VO[:, b, 4 * c:4 * c + n, :].rearrange("p q d -> p (q d)"),
                                     TP[g % 2][:, 0:n * P], ACT.Copy).then_inc(vo_used, 1)
            softmax_exp(1, 1)
            copy_probs(0)
            pair_turn(1)
            with act.Fori(2, PAIR_TURNS) as i:
                pair_turn(i)
            copy_probs(TILES - 1)
            pass_rows(PAIR_TURNS - 1)
            weigh_choices(PAIR_TURNS - 1)

            def slot_hi(s, u):
                act.wait_ge(sT_ready, s + 1)
                if from_(s, 2):
                    act.wait_ge(sup_ready, s - 1)
                nc.scalar.activation(XT_hi[u][:, :], XP[:, 0:P], ACT.Copy).then_inc(shi_ready, 1)

            def silu(s, u):
                act.wait_ge(sgate_ready, s + 1)
                if from_(s, 2):
                    act.wait_ge(he_ready, s - 1)
                nc.scalar.activation(SG[:, u, :], GP[u][:, :], ACT.Silu).then_inc(silu_ready, 1)

            def slot_turn(s, k, u):
                act.wait_ge(heT_ready, s + 1)
                if from_(s, 2):
                    act.wait_ge(ye_ready, s - 1)
                nc.scalar.activation(HT[:, u, :, :].rearrange("p q d -> p (q d)"), HP[u][:, :],
                                     ACT.Copy).then_inc(heT_copied, 1)
                if slots_ahead(s, 1):
                    silu(s + 1, 1 - u)
                if slots_ahead(s, 2):
                    slot_hi(s + 2, u)
                act.wait_ge(ye_ready, s + 1)
                if from_(s, RIN):
                    act.wait_ge(yo_out[k], s // RIN * 16)
                nc.scalar.activation(YO[:, k, :], DP[:, 0:D], ACT.Copy,
                                     scale=RT[:, k, D + 1:D + 2]).then_inc(yo_ready, 1)

            slot_hi(0, 0)
            silu(0, 0)
            slot_hi(1, 1)
            slot_loop(act, slot_turn)

        @block.vector
        def _(dve):
            steps = Steps(dve, dve_steps)
            dve.wait_ge(ld_x, 16)
            for t in range(TILES):
                last = nc.vector.bn_stats(stats[:, t, :], X[:, t, :])
            steps.link(last)
            for t in range(TILES):
                last = nc.vector.bn_aggr(mv[:, t, :], stats[:, t, :])
            steps.link(last)
            nc.vector.tensor_scalar(veps[:, :], mv[:, :, 1], 1.0 + EPS, EPS * EPS, ALU.mult,
                                    ALU.add).then_inc(xvar_ready, 1)
            dve.wait_ge(ld_ctx, 16)
            for b in range(B):
                last = nc.vector.bn_stats(cstats[:, b, :], CTX[:, b, :])
            steps.link(last)
            for b in range(B):
                last = nc.vector.bn_aggr(cmv[:, b, :], cstats[:, b, :])
            steps.link(last)
            nc.vector.tensor_scalar(cveps[:, :], cmv[:, :, 1], EPS, None, ALU.add).then_inc(cvar_ready, 1)
            dve.wait_ge(f1hi_ready, 1)
            nc.vector.tensor_tensor(F1_lo[:, :], F1, F1_hi[:, :].bitcast(F32), ALU.subtract).then_inc(f1_split, 1)

            def xhat(t, u):
                if from_(t, 2):
                    dve.wait_ge(xT_ready, t - 1)
                nc.vector.tensor_scalar(XH[:, u, :], X[:, t, :], mv[:, t, 0:1], rx[:, bass.ds(t, 1)], ALU.subtract,
                                        ALU.mult).then_inc(xh_ready, 1)

            def split_xn(t, u):
                dve.wait_ge(xn_ready, t + 1)
                if from_(t, 2):
                    dve.wait_ge(fu_ready, t - 1)
                    dve.wait_ge(xn_kept, t - 1)
                steps.link(nc.vector.tensor_copy(XN_hi[u][:, :], XN[:, u, :]))
                nc.vector.tensor_tensor(XN_lo[u][:, :], XN[:, u, :], XN_hi[u][:, :].bitcast(F32),
                                        ALU.subtract).then_inc(xn_split, 1)

            dve.wait_ge(xrs_ready, 1)
            xhat(0, 0)
            xhat(1, 1)
            split_xn(0, 0)
            split_xn(1, 1)
            dve.wait_ge(crs_ready, 1)
            for b in range(B):
                nc.vector.tensor_scalar(CHAT[:, b, :], CTX[:, b, :], cmv[:, b, 0:1], rc[:, b:b + 1], ALU.subtract,
                                        ALU.mult).then_inc(chat_ready, 1)
            dve.wait_ge(tg_ready, 1)

            def add_ff(t):
                dve.wait_ge(ff_ready, t + 1)
                nc.vector.scalar_tensor_tensor(X[:, t, :], DP[:, 0:D], tg[:, 0:1], X[:, t, :], ALU.mult,
                                               ALU.add).then_inc(ff_added, 1)

            def ff_turn(t, u):
                if ahead(t, 2):
                    xhat(t + 2, u)
                dve.wait_ge(fsilu_ready, t + 1)
                dve.wait_ge(fu_ready, t + 1)
                if from_(t, 2):
                    dve.wait_ge(fhT_ready, t - 1)
                nc.vector.tensor_tensor(HH[:, u, :], SG[:, u, :], UP[u][:, :], ALU.mult).then_inc(fh_ready, 1)
                if ahead(t, 2):
                    split_xn(t + 2, u)
                if from_(t, 1):
                    add_ff(t - 1)

            ff_turn(0, 0)
            ff_turn(1, 1)
            with dve.Fori(1, PAIR_TURNS - 1) as i:
                steps.enter(i, 1, 2)
                for u in range(2):
                    ff_turn(2 * i + u, u)
            steps.leave(PAIR_TURNS - 2)
            ff_turn(TILES - 2, 0)
            ff_turn(TILES - 1, 1)

            nc.vector.memset(kdiag[:, :, :, :], 0.0)
            steps.link(nc.vector.memset(vpad[:, :, :], 0.0))
            add_ff(TILES - 1)
            dve.wait_ge(kv_ready, 1)
            kv = XP[:, 0:2 * B * J].rearrange("p (w b j) -> p w b j", w=2, b=B)
            for c in range(2):
                rws = slice(DH * c, DH * (c + 1))
                nc.vector.tensor_scalar(kdiag[rws, :, c, :], kv[rws, 0], DH ** -0.5, None, ALU.mult)
                last = nc.vector.tensor_copy(vpad[rws, :, P + J * c:P + J * (c + 1)], kv[rws, 1])
            last.then_inc(kv_used, 1)
            for p in range(PAIRS):
                dve.wait_ge(ahi_ready, p + 1)
                cs = slice(2 * J * p, 2 * J * (p + 1))
                nc.vector.tensor_tensor(A_lo[:, :, cs], bank[p % 5][:, 0:B * 2 * J].rearrange("p (b c) -> p b c", b=B),
                                        A_hi[:, :, cs].bitcast(F32), ALU.subtract).then_inc(a_used, 1)

            S4 = [SC[g][:, 0:(HB if g < 2 else TAILH) * J].rearrange("p (h j) -> p h j", j=J) for g in range(3)]
            heads = [(0, HB), (HB, 2 * HB), (2 * HB, H)]

            def shift(t, u):
                dve.wait_ge(scores_ready, t + 1)
                for g in (2, 0, 1):
                    a, b = heads[g]
                    last = nc.vector.tensor_reduce(nM[:, u, a:b], S4[g], AX_X, ALU.max, negate=True)
                last.then_inc(nmax_ready, 1)
                dve.wait_ge(nmax_ready, t + 1)
                if from_(t, 2):
                    dve.wait_ge(tp_ready, 3 * (t - 1))
                for g in range(2):
                    a, b = heads[g]
                    last = nc.vector.tensor_tensor(PR[:, u, a * J:b * J].rearrange("p (h j) -> p h j", j=J), S4[g],
                                                   nM[:, u, a:b].unsqueeze(2).to_broadcast([P, b - a, J]), ALU.add)
                last.then_inc(shift_ready, 1)

            def sums(t, u):
                dve.wait_ge(exp_ready, t + 1)
                steps.link(nc.vector.tensor_reduce(RS[:, u, :], PR[:, u, :].rearrange("p (h j) -> p h j", j=J),
                                                   AX_X, ALU.add))
                nc.vector.reciprocal(RI[:, u, :], RS[:, u, :]).then_inc(rsum_ready, 1)

            def residual(i):
                dve.wait_ge(acc_ready, 2 * i + 2)
                nc.vector.scalar_tensor_tensor(X2[:, bass.ds(2 * i, 2), :], acc_ps, tg[:, 0:1],
                                               X[:, bass.ds(2 * i, 2), :], ALU.mult, ALU.add).then_inc(acc_read, 1)
                dve.drain()
                for n in range(2):
                    nc.vector.bn_stats(st2[:, n, :], X2[:, bass.ds(2 * i + n, 1), :].rearrange("p a d -> p (a d)"))
                dve.drain()
                for n in range(2):
                    last = nc.vector.bn_aggr(mv2[:, n, :], st2[:, n, :])
                steps.link(last)
                nc.vector.tensor_scalar(ve2[:, :], mv2[:, :, 1], EPS, None, ALU.add).then_inc(var2_ready, 1)

            def normed(i):
                dve.wait_ge(r2_ready, i + 1)
                if from_(i, 1):
                    dve.wait_ge(row_copied, i)
                for n in range(2):
                    last = nc.vector.tensor_scalar(YB[:, n, :], X2[:, bass.ds(2 * i + n, 1), :].rearrange("p a d -> p (a d)"),
                                                   mv2[:, n, 0:1], r2[:, n:n + 1], ALU.subtract, ALU.mult)
                last.then_inc(y_ready, 1)

            def choose(i):
                dve.wait_ge(logits_ready, i + 1)
                nc.vector.tensor_tensor(LG[:, :, :], lg_ps, GB[:, :].unsqueeze(1).to_broadcast([P, 2, E]), ALU.add)
                dve.drain()
                for n in range(2):
                    last = nc.vector.max(MX[:, n, :], LG[:, n, :])
                steps.link(last)
                nc.vector.tensor_scalar(ntop[:, :], MX[:, :, 0], -1.0, None, ALU.mult).then_inc(ntop_ready, 1)
                for n in range(2):
                    last = nc.vector.max_index(IX[:, n, :], MX[:, n, :], LG[:, n, :])
                steps.link(last)
                steps.link(nc.vector.tensor_copy(IXF[:, :, :], IX[:, :, 0:2]))
                iota4 = iota_e[:, :].unsqueeze(1).to_broadcast([P, 2, E]).unsqueeze(1).to_broadcast([P, 2, 2, E])
                steps.link(nc.vector.tensor_tensor(pick[:, :, :, :], iota4,
                                                   IXF[:, :, :].unsqueeze(3).to_broadcast([P, 2, 2, E]), ALU.is_equal))
                steps.link(nc.vector.tensor_tensor(Ms[:, :, :], pick[:, :, 0, :], pick[:, :, 1, :], ALU.add))
                steps.link(nc.vector.tensor_tensor(Macc[:, bass.ds(2 * i + 1, 1), :], Macc[:, bass.ds(2 * i, 1), :],
                                                   Ms[:, 0:1, :], ALU.add))
                nc.vector.tensor_tensor(Macc[:, bass.ds(2 * i + 2, 1), :], Macc[:, bass.ds(2 * i + 1, 1), :],
                                        Ms[:, 1:2, :], ALU.add).then_inc(picks_ready, 1)
                dve.wait_ge(e2_ready, i + 1)
                steps.link(nc.vector.reciprocal(esinv[:, :], esum[:, :]))
                if from_(i, 1):
                    dve.wait_ge(rows_out, i * 64)
                for n in range(2):
                    nc.vector.tensor_scalar(rows[:, n, :, D + 1:D + 2].rearrange("p k a -> p (k a)"), e2[:, n, :],
                                            esinv[:, n:n + 1], tg[:, 1:2], ALU.mult, ALU.mult)
                dve.wait_ge(rank_ready, i + 1)
                nc.vector.tensor_tensor(rkb[:, :, :], rk_ps, base_e[:, :].unsqueeze(1).to_broadcast([P, 2, E]),
                                        ALU.add).then_inc(rank_read, 1)
                dve.wait_ge(rank_read, i + 1)
                steps.link(nc.vector.tensor_tensor(prod[:, :, :, :], pick[:, :, :, :],
                                                   rkb[:, :, :].unsqueeze(2).to_broadcast([P, 2, 2, E]), ALU.mult))
                with nc.allow_low_precision("slot numbers are whole numbers below 2^24"):
                    nc.vector.tensor_reduce(slot[:, :, :], prod[:, :, :, :], AX_X, ALU.add).then_inc(slots_ready, 1)

            def pair_turn(i):
                shift(2 * i, 0)
                sums(2 * i, 0)
                if from_(i, 1):
                    residual(i - 1)
                shift(2 * i + 1, 1)
                if from_(i, 1):
                    normed(i - 1)
                sums(2 * i + 1, 1)
                if from_(i, 1):
                    choose(i - 1)

            pair_turn(0)
            dve.wait_ge(ld_gw, 32)
            dve.wait_ge(consts, 3)
            pair_turn(1)
            with dve.Fori(2, PAIR_TURNS) as i:
                steps.enter(i, 2, 11)
                pair_turn(i)
            steps.leave(PAIR_TURNS - 2)
            residual(PAIR_TURNS - 1)
            normed(PAIR_TURNS - 1)
            choose(PAIR_TURNS - 1)

            dve.wait_ge(counts_ready, 1)
            with nc.allow_low_precision("counts are whole numbers below 2^24"):
                steps.link(nc.vector.tensor_scalar(T8u[:, :], ct_ps, float(P - 1), None, ALU.add))
                steps.link(nc.vector.tensor_scalar(T8u[:, :], T8u[:, :], 7, None, ALU.logical_shift_right))
                steps.link(nc.vector.tensor_copy(Tn[:, :], T8u[:, :]))
                steps.link(nc.vector.tensor_tensor(TT[:, :, :], tri[:, :, :], Tn[:, :].unsqueeze(1).to_broadcast([1, E, E]), ALU.mult))
                steps.link(nc.vector.tensor_reduce(Tend[:, :], TT[:, :, :], AX_X, ALU.add))
                steps.link(nc.vector.tensor_tensor(GE[:, :, :], iota_s[:, :].unsqueeze(2).to_broadcast([1, SLOT_TILES, E]),
                                                   Tend[:, :].unsqueeze(1).to_broadcast([1, SLOT_TILES, E]), ALU.is_ge))
                steps.link(nc.vector.tensor_reduce(es[:, :], GE[:, :, :], AX_X, ALU.add))
                steps.link(nc.vector.tensor_tensor(GT[:, :, :], GE[:, :, :], Tn[:, :].unsqueeze(1).to_broadcast([1, SLOT_TILES, E]), ALU.mult))
                steps.link(nc.vector.tensor_reduce(ts_[:, :], GT[:, :, :], AX_X, ALU.add))
                steps.link(nc.vector.tensor_tensor(rowb[:, :], iota_s[:, :], ts_[:, :], ALU.subtract))
                steps.link(nc.vector.tensor_scalar(rowb[:, :], rowb[:, :], float(P), None, ALU.mult))
                nc.vector.tensor_scalar(expert_of[:, :], es[:, :], float(E - 1), None, ALU.min)
                nc.vector.scalar_tensor_tensor(row_of[:, :], es[:, :], float(CAP), rowb[:, :], ALU.mult,
                                               ALU.add).then_inc(tables_ready, 1)

            def slot_lo(s, u):
                dve.wait_ge(shi_ready, s + 1)
                nc.vector.tensor_tensor(XT_lo[u][:, :], XP[:, 0:P], XT_hi[u][:, :].bitcast(F32),
                                        ALU.subtract).then_inc(s_split, 1)

            def gate_up(s, u):
                dve.wait_ge(silu_ready, s + 1)
                dve.wait_ge(sup_ready, s + 1)
                if from_(s, 2):
                    dve.wait_ge(heT_ready, s - 1)
                nc.vector.tensor_tensor(HH[:, u, :], SG[:, u, :], UP[u][:, :], ALU.mult).then_inc(he_ready, 1)

            def slot_turn(s, k, u):
                if slots_ahead(s, 1):
                    gate_up(s + 1, 1 - u)
                if slots_ahead(s, 2):
                    slot_lo(s + 2, u)

            slot_lo(0, 0)
            gate_up(0, 0)
            slot_lo(1, 1)
            slot_loop(dve, slot_turn)

            dve.wait_ge(back_in, 16)
            steps.link(nc.vector.tensor_tensor(X2[:, :, :], X2[:, :, :], back[:, :, 0:D], ALU.add))
            nc.vector.tensor_tensor(X2[:, :, :], X2[:, :, :], back[:, :, D:2 * D], ALU.add).then_inc(osum_ready, 1)

        @block.tensor
        def _(pe):
            def mm3(o, l_hi, l_lo, r_hi, r_lo):
                nc.tensor.matmul(o, l_hi, r_hi, start=True, stop=False)
                nc.tensor.matmul(o, l_lo, r_hi, start=False, stop=False)
                return nc.tensor.matmul(o, l_hi, r_lo, start=False, stop=True)

            pe.wait_ge(consts, 2)

            def transpose_xhat(t, u):
                pe.wait_ge(xh_ready, t + 1)
                if from_(t, 1):
                    pe.wait_ge(xn_ready, t)
                nc.tensor.transpose(XP[:, 0:P], XH[:, u, :], identf[:, :]).then_inc(xT_ready, 1)

            def transpose_h(t, u):
                pe.wait_ge(fh_ready, t + 1)
                if from_(t, 2):
                    pe.wait_ge(fhT_copied, t - 1)
                for c in range(FC):
                    last = nc.tensor.transpose(HP[u][:, c * P:(c + 1) * P], HH[:, u, c * P:(c + 1) * P], identf[:, :])
                last.then_inc(fhT_ready, 1)

            def down(t, u):
                pe.wait_ge(fhT_copied, t + 1)
                if from_(t, 1):
                    pe.wait_ge(ff_added, t)
                for c in range(FC):
                    last = nc.tensor.matmul(DP[:, 0:D], HT[:, u, c, :], F2[:, c, :], start=c == 0, stop=c == FC - 1)
                last.then_inc(ff_ready, 1)

            def ff_turn(t, u):
                if from_(t, 1):
                    transpose_h(t - 1, 1 - u)
                pe.wait_ge(xn_split, t + 1)
                if from_(t, 2):
                    pe.wait_ge(fh_ready, t - 1)
                mm3(GP[u][:, :], XN_hi[u][:, :], XN_lo[u][:, :], F1_hi[:, FF:2 * FF], F1_lo[:, FF:2 * FF]).then_inc(fg_ready, 1)
                mm3(UP[u][:, :], XN_hi[u][:, :], XN_lo[u][:, :], F1_hi[:, 0:FF], F1_lo[:, 0:FF]).then_inc(fu_ready, 1)
                if ahead(t, 2):
                    transpose_xhat(t + 2, u)
                if from_(t, 1):
                    down(t - 1, 1 - u)

            transpose_xhat(0, 0)
            transpose_xhat(1, 1)
            pe.wait_ge(f1_split, 1)
            pe.wait_ge(ld_f2, 16)
            tile_loop(pe, ff_turn)
            pe.wait_ge(chat_ready, B)
            for b in range(B):
                last = nc.tensor.transpose(XP[:, b * J:(b + 1) * J], CHAT[:, b, :], identf[0:J, 0:J])
            last.then_inc(cT_ready, 1)
            transpose_h(TILES - 1, 1)
            down(TILES - 1, 1)

            pe.wait_ge(ld_wq, 16)
            for g in range(2):
                for q in range(4):
                    last = nc.tensor.transpose(GP[g][:, q * P:(q + 1) * P], WQ[:, (4 * g + q) * P:(4 * g + q + 1) * P],
                                               identf[:, :])
                last.then_inc(wqT_ready, 1)
            pe.wait_ge(ld_wkv, 32)
            pe.wait_ge(cn_ready, 1)
            for w in range(2):
                last = nc.tensor.matmul(XP[:, w * B * J:(w + 1) * B * J], WKV2[:, w, :, :].rearrange("p c d -> p (c d)"),
                                        CN[:, :], start=True, stop=True)
            last.then_inc(kv_ready, 1)
            pe.wait_ge(kv_used, 1)
            pe.wait_ge(wqT_used, 2)
            for p in range(PAIRS):
                if p >= 5:
                    pe.wait_ge(a_used, p - 4)
                nc.tensor.matmul(bank[p % 5][:, 0:B * 2 * J], WQT[:, p, :], kdiag[:, :, :, :].rearrange("p b c j -> p (b c j)"),
                                 start=True, stop=True).then_inc(a_ready, 1)

            def scores(t, u, b):
                pe.wait_ge(xn_held, t + 1)
                if from_(t, 1):
                    pe.wait_ge(shift_ready, t)
                    pe.wait_ge(exp_ready, t)
                for g, (a, e) in enumerate(((0, HB), (HB, 2 * HB), (2 * HB, H))):
                    n = (e - a) * J
                    hi = A_hi[:, bass.ds(b, 1), a * J:e * J].rearrange("p a c -> p (a c)")
                    lo = A_lo[:, bass.ds(b, 1), a * J:e * J].rearrange("p a c -> p (a c)")
                    last = mm3(SC[g][:, 0:n], XN_hi[u][:, :], XN_lo[u][:, :], hi, lo)
                last.then_inc(scores_ready, 1)

            def attend(t, u, b):
                def turn(q):
                    if q == 0:
                        pe.wait_ge(probs_ready, t + 1)
                    if q < 2:
                        if from_(t, 1):
                            pe.wait_ge(tp_copied, 3 * t)
                    else:
                        pe.wait_ge(tp_copied, 3 * t + 1)
                    for n, c in enumerate(range(4 * q, min(4 * q + 4, CH))):
                        s = PR[:, u, c * P:min((c + 1) * P, HJ)]
                        w = s.shape[1]
                        last = nc.tensor.transpose(TP[q % 2][0:w, n * P:(n + 1) * P], s, identf[:, :])
                    last.then_inc(tp_ready, 1)

                def share(q):
                    pe.wait_ge(tp_copied, 3 * t + q + 1)
                    if q == 0 and u == 0 and from_(t, 2):
                        pe.wait_ge(acc_read, t // 2)
                    for c in range(4 * q, min(4 * q + 4, CH)):
                        k = LASTC if c == CH - 1 else P
                        last = nc.tensor.matmul(acc_ps[:, u, :], PT[0:k, c, :],
                                                VO[0:k, bass.ds(b, 1), c, :].rearrange("p a d -> p (a d)"),
                                                start=c == 0, stop=c == CH - 1)
                    return last

                turn(0)
                turn(1)
                share(0)
                turn(2)
                share(1)
                share(2).then_inc(acc_ready, 1)

            def route(i):
                pe.wait_ge(y_ready, i + 1)
                if from_(i, 1):
                    pe.wait_ge(slots_ready, i)
                for n in range(2):
                    last = nc.tensor.transpose(y_T[:, n, :], YB[:, n, :], identf[:, :])
                last.then_inc(yT_ready, 1)
                pe.wait_ge(yT_copied, i + 1)
                for n in range(2):
                    last = nc.tensor.matmul(lg_ps[:, n, :], YT[:, n, :], GW[:, :], start=True, stop=True)
                last.then_inc(logits_ready, 1)

            def ranks(i):
                pe.wait_ge(picks_ready, i + 1)
                if from_(i, 1):
                    pe.wait_ge(rank_read, i)
                nc.tensor.matmul(rk_ps, lower_b[:, :], Ms[:, :, :], start=True, stop=False)
                nc.tensor.matmul(rk_ps, ones_b[:, :], Macc[:, bass.ds(2 * i, 2), :], start=False,
                                 stop=True).then_inc(rank_ready, 1)

            def pair_turn(i, b, b_before):
                scores(2 * i, 0, b)
                if from_(i, 1):
                    attend(2 * i - 1, 1, b_before)
                scores(2 * i + 1, 1, b)
                if from_(i, 1):
                    route(i - 1)
                attend(2 * i, 0, b)
                if from_(i, 1):
                    ranks(i - 1)

            pe.wait_ge(a_used, PAIRS)
            scores(0, 0, 0)
            pe.wait_ge(ld_wo, 16)
            for g in range(6):
                b, c4 = divmod(g, 3)
                if g >= 2:
                    pe.wait_ge(vo_used, g - 1)
                for c in range(4 * c4, min(4 * c4 + 4, CH)):
                    crossed = [p for p in range(PAIRS) if 0 < P + P * c - 2 * J * p < P + 2 * J]
                    for p in crossed:
                        at = P + P * c - 2 * J * p
                        last = nc.tensor.matmul(TP[g % 2][:, (c - 4 * c4) * P:(c - 4 * c4 + 1) * P],
                                                vpad[:, b, at:at + P], WO[:, p, :],
                                                start=p == crossed[0], stop=p == crossed[-1])
                last.then_inc(vo_ready, 1)
            scores(1, 1, 0)
            pe.wait_ge(vo_used, 6)
            attend(0, 0, 0)
            pe.wait_ge(ld_gw, 32)
            pe.wait_ge(consts, 3)
            pair_turn(1, 2 // PER_BATCH, 1 // PER_BATCH)
            with pe.Fori(2, PAIR_TURNS) as i:
                pair_turn(i, 2 * i // PER_BATCH, (2 * i - 1) // PER_BATCH)
            attend(TILES - 1, 1, B - 1)
            route(PAIR_TURNS - 1)
            ranks(PAIR_TURNS - 1)
            pe.wait_ge(rank_read, PAIR_TURNS)
            nc.tensor.matmul(ct_ps, ones_b[:, 0:1], Macc[:, TILES, :], start=True, stop=True).then_inc(counts_ready, 1)

            pe.wait_ge(tables_ready, 1)
            pe.wait_ge(w_split, E)
            pe.wait_ge(ld_w2, E * 16)

            def transpose_slots(s, k, u):
                pe.wait_ge(rt_in[k], (s // RIN + 1) * 16)
                if from_(s, 1):
                    pe.wait_ge(s_split, s)
                nc.tensor.transpose(XP[:, 0:P], RT[:, k, 0:D], identf[:, :]).then_inc(sT_ready, 1)

            def slot_expert(s):
                return pe.value_load(expert_of[0:1, bass.ds(s, 1)], min_val=0, max_val=E - 1)

            def slot_gate_up(s, u, e):
                pe.wait_ge(s_split, s + 1)
                if from_(s, 2):
                    pe.wait_ge(he_ready, s - 1)
                for n, (o, done) in enumerate(((GP, sgate_ready), (UP, sup_ready))):
                    cs = slice(n * F, (n + 1) * F)
                    mm3(o[u][:, :], XT_hi[u][:, :], XT_lo[u][:, :],
                        W13_hi[:, bass.ds(e, 1), cs].rearrange("p a f -> p (a f)"),
                        W13_lo[:, bass.ds(e, 1), cs].rearrange("p a f -> p (a f)")).then_inc(done, 1)

            def slot_turn(s, k, u):
                e = slot_expert(s)
                e_next = slot_expert(s + 1) if slots_ahead(s, 1) else None
                pe.wait_ge(he_ready, s + 1)
                if from_(s, 2):
                    pe.wait_ge(heT_copied, s - 1)
                for c in range(FC):
                    last = nc.tensor.transpose(HP[u][:, c * P:(c + 1) * P], HH[:, u, c * P:(c + 1) * P], identf[:, :])
                last.then_inc(heT_ready, 1)
                if slots_ahead(s, 1):
                    slot_gate_up(s + 1, 1 - u, e_next)
                if slots_ahead(s, 2):
                    transpose_slots(s + 2, (k + 2) % RIN, u)
                pe.wait_ge(heT_copied, s + 1)
                if from_(s, 1):
                    pe.wait_ge(yo_ready, s)
                for c in range(FC):
                    last = nc.tensor.matmul(DP[:, 0:D], HT[:, u, c, :],
                                            W2[:, bass.ds(e, 1), c * P:(c + 1) * P].rearrange("p a f -> p (a f)"),
                                            start=c == 0, stop=c == FC - 1)
                last.then_inc(ye_ready, 1)

            transpose_slots(0, 0, 0)
            slot_gate_up(0, 0, slot_expert(0))
            transpose_slots(1, 1, 1)
            slot_loop(pe, slot_turn)


_INS = ['x', 'ctx_1024', 'g_xattn', 'g_ffn', 'L0_xattn_ln_g', 'L0_xattn_ln_b', 'L0_xattn_cln_g', 'L0_xattn_cln_b',
        'L0_xattn_Wq', 'L0_xattn_Wkv', 'L0_xattn_Wo', 'L0_xattn_Wff1', 'L0_xattn_Wff2', 'L0_ffn_gate_w',
        'L0_ffn_gate_b', 'L0_ffn_w1', 'L0_ffn_w3', 'L0_ffn_w2']
_OUTS = [((2, 512, 128), 'float32')]


def kernel(**inputs):
    import numpy as _np
    import concourse.bacc as _bacc
    from concourse import mybir as _mybir
    from concourse.bass_utils import run_bass_kernel_spmd as _run

    nc = _bacc.Bacc("TRN2", target_bir_lowering=False, num_devices=1)
    arrays, args = {}, []
    for name in _INS:
        a = _np.ascontiguousarray(inputs[name])
        arrays[f"in_{name}_dram"] = a
        args.append(nc.dram_tensor(f"in_{name}_dram", a.shape, _mybir.dt.from_np(a.dtype), kind="ExternalInput").ap())
    for i, (shape, dtype) in enumerate(_OUTS):
        dt = _mybir.dt.from_np(_np.dtype(dtype))
        args.append(nc.dram_tensor(f"out_{i}_dram", shape, dt, kind="ExternalOutput").ap())
    gated_block_kernel(nc, *args)
    r = _run(nc, [arrays], core_ids=[0])
    return r.results[0]["out_0_dram"]
```

```python
from contextlib import ExitStack

import concourse.bass as bass
from concourse import mybir

ALU = mybir.AluOpType
ACT = mybir.ActivationFunctionType
AX_X = mybir.AxisListType.X
F32 = mybir.dt.float32
F32R = mybir.dt.float32r
BF16 = mybir.dt.bfloat16
U32 = mybir.dt.uint32
I32 = mybir.dt.int32
P = 128


class Steps:

    def __init__(self, engine, semaphore):
        self.engine, self.semaphore, self.count = engine, semaphore, 0

    def link(self, instruction):
        self.did(instruction)
        self.wait()

    def did(self, instruction):
        instruction.then_inc(self.semaphore, 1)
        self.count += 1

    def wait(self):
        self.engine.wait_ge(self.semaphore, self.count)


def gated_block_kernel(nc, x, ctx_in, g_xattn, g_ffn, ln_g, ln_b, cln_g, cln_b, wq, wkv, wo, wff1, wff2,
                       gate_w, gate_b, w1, w3, w2, out):
    B, N, D = x.shape
    J = ctx_in.shape[1]
    INNER = wq.shape[1]
    DH = wkv.shape[1] // 2
    H = INNER // DH
    FF = wff2.shape[0]
    E, _, F = w1.shape
    EPS = 1e-5
    TILES = B * N // P
    PER_BATCH = N // P
    HJ = H * J
    PAIRS = H // 2
    CH = -(-HJ // P)
    LASTC = HJ - (CH - 1) * P
    HEADS = [(0, 6), (6, H - 6), (H - 6, H)]
    TAIL = HEADS[2][0]
    GROUPS = [(0, 3), (3, 7), (7, CH)]
    SHARED = H * 5 // 8
    FC = F // P
    CAP = TILES * P
    SLOT_TILES = (2 * B * N - E) // P + E
    SPARE = SLOT_TILES - 2 * B * N // P
    assert FF // P == 4 and TAIL // 2 < H // 2
    QUARTERS = [slice(t, t + TILES // 4) for t in range(0, TILES, TILES // 4)]
    REGION = E * CAP + SPARE * P
    ROW = D + 2
    RETURN = 2 * B * N
    assert E - E // 2 == 4 and B == 2 and TILES == 2 * FF // P and H // 2 == TILES and E == TILES
    assert D == P and 2 * DH == P and F == 4 * P and FF == 4 * P and max(e - a for a, e in HEADS) * J <= 512 and TILES % 2 == 0

    dispatched = nc.dram_tensor("dispatched", (REGION, ROW), F32, kind="Internal").ap()
    returned = nc.dram_tensor("returned", (RETURN, D), F32, kind="Internal").ap()

    with ExitStack() as ctx:
        def sb(name, shape, dt=F32):
            return ctx.enter_context(nc.sbuf_tensor(name, shape, dt))

        def sem(name):
            return ctx.enter_context(nc.semaphore(name))

        X = sb("X", [P, TILES, D])
        X2 = sb("X2", [P, TILES, D])
        WO = X2[:, :, :]
        CTX = sb("CTX", [J, B, D])
        CHAT = sb("CHAT", [J, B, D])
        CN = sb("CN", [P, B * J])
        WKV2 = sb("WKV2", [P, 2, 2, DH])
        kdiag = sb("kdiag", [P, B, 2, J])
        VP = P + 2 * J + P
        vpad = sb("vpad", [P, B, VP])
        early = sb("early", [P, 2 * INNER])
        WQ = early[:, 0:INNER]
        WQT = early[:, INNER:2 * INNER].rearrange("p (q d) -> p q d", d=D)
        PT = early[:, 0:CH * P].rearrange("p (q d) -> p q d", d=P)
        PR = sb("PR", [P, 2, HJ])
        F1 = PR[:, 0, 0:2 * FF]
        XN = PR[:, 1, 0:B * PER_BATCH * P].rearrange("p (b c) -> p b c", b=B)
        back = PR[:, :, :].rearrange("p u c -> p (u c)")[:, 0:TILES * 2 * D].rearrange("p (t c) -> p t c", c=2 * D)
        A_hi = sb("A_hi", [P, B, HJ], F32R)
        A_lo = sb("A_lo", [P, B, HJ], F32R)
        VO = sb("VO", [P, B, CH, D])
        F1_hi = sb("F1_hi", [P, 2 * FF], F32R)
        F1_lo = sb("F1_lo", [P, 2 * FF], F32R)
        F2 = sb("F2", [P, FF // P, D])
        lng = sb("lng", [P, 4])
        gates = sb("gates", [P, 2])
        tg = sb("tg", [P, 2])
        GW = sb("GW", [P, E])
        GB = sb("GB", [P, E])
        half = sb("half", [P, TILES])
        stats = sb("stats", [P, TILES, 6])
        mv = sb("mv", [P, TILES, 2])
        veps = sb("veps", [P, TILES])
        rx = sb("rx", [P, TILES])
        cstats = sb("cstats", [J, B, 6])
        cmv = sb("cmv", [J, B, 2])
        cveps = sb("cveps", [J, B])
        rc = sb("rc", [J, B])
        identf = sb("identf", [P, P])
        ones_b = sb("ones_b", [P, P], BF16)
        lower_b = sb("lower_b", [P, P], BF16)
        iota_e = sb("iota_e", [P, E], U32)
        base_e = sb("base_e", [1, E])
        dest0 = sb("dest0", [P, 2, 2], U32)
        pair_step = sb("pair_step", [P, 2, 2], U32)
        padrow = sb("padrow", [P, ROW])
        xnT_hi = sb("xnT_hi", [P, TILES, P], F32R)
        xnT_lo = sb("xnT_lo", [P, TILES, P], F32R)
        XT_hi = [sb(f"XT_hi{u}", [P, P], F32R) for u in range(2)]
        XT_lo = [sb(f"XT_lo{u}", [P, P], F32R) for u in range(2)]
        nM = sb("nM", [P, 2, H])
        RS = sb("RS", [P, 2, H])
        RI = sb("RI", [P, 2, H])
        SG = sb("SG", [P, 2, F])
        HC = sb("HC", [P, FF // P, PER_BATCH * P])
        HH = HC[:, 0:2, :]
        HT = HC[:, 2:4, :].rearrange("p u (q d) -> p u q d", d=P)
        st2 = sb("st2", [P, 2, 6])
        mv2 = sb("mv2", [P, 2, 2])
        ve2 = sb("ve2", [P, 2])
        r2 = sb("r2", [P, 2])
        YB = sb("YB", [P, 2, D])
        YT = sb("YT", [P, 2, P])
        rows = sb("rows", [P, 2, 2, ROW])
        last_rows = [v[:, 0:4 * ROW].rearrange("p (t k c) -> p t k c", t=2, k=2)
                     for v in (HH[:, :, :].rearrange("p u f -> p (u f)"), HT[:, :, :, :].rearrange("p u q d -> p (u q d)"))]
        LG = sb("LG", [P, 2, E])
        MX = sb("MX", [P, 2, 8])
        IX = sb("IX", [P, 2, 8], U32)
        ntop = sb("ntop", [P, 2])
        e2 = sb("e2", [P, 2, 2])
        esum = sb("esum", [P, 2])
        esinv = sb("esinv", [P, 2])
        pick = sb("pick", [P, 2, 2, E], BF16)
        picked = sb("picked", [P, E], BF16)
        before = sb("before", [P, E], BF16)
        prod = sb("prod", [P, 2, 2, E])
        slot = sb("slot", [P, 2, 2], U32)
        last_slot = [sb(f"last_slot{n}", [P, 2, 2], U32) for n in range(2)]
        T8u = sb("T8u", [1, E], U32)
        Tn = sb("Tn", [1, E])
        tri = sb("tri", [1, E, E])
        TT = sb("TT", [1, E, E])
        Tend = sb("Tend", [1, E])
        iota_s = sb("iota_s", [1, SLOT_TILES])
        GE = sb("GE", [1, SLOT_TILES, E])
        GT = sb("GT", [1, SLOT_TILES, E])
        es = sb("es", [1, SLOT_TILES])
        ts_ = sb("ts_", [1, SLOT_TILES])
        rowb = sb("rowb", [1, SLOT_TILES])
        expert_of = sb("expert_of", [1, SLOT_TILES], I32)
        row_of = sb("row_of", [1, SLOT_TILES], I32)
        WS = sb("WS", [P, 2, 2 * F])
        W13_hi = sb("W13_hi", [P, E, 2 * F], F32R)
        W13_lo = sb("W13_lo", [P, E, 2 * F], F32R)
        W2 = sb("W2", [P, E, F])
        W2_stage = W2[:, :, :].rearrange("p e f -> p (e f)").rearrange("p (e f) -> p e f", f=2 * F)
        VO_stage = VO[:, :, :, :].rearrange("p b c d -> p (b c d)")[:, 0:2 * 2 * F].rearrange("p (e f) -> p e f", f=2 * F)
        STAGES = [(0, 2, WS), (2, 2 + E // 2, W2_stage), (2 + E // 2, E, VO_stage)]
        RIN = 6
        RT = WS[:, 0, 0:RIN * ROW].rearrange("p (k c) -> p k c", c=ROW)
        YO = WS[:, 1, 0:RIN * D].rearrange("p (k c) -> p k c", c=D)

        bank = [ctx.enter_context(nc.psum_tensor(f"bank{i}", [P, 512], F32)) for i in range(8)]
        GP, UP, FP, XP, CP = bank[0:2], bank[2:4], bank[4], bank[6], bank[7]
        QP = [bank[4], bank[5]]
        A_PS = [bank[5], bank[7]]
        SC, TP, AP, YP = bank[0:3], bank[3:5], bank[5:7], bank[7]
        VO_PS = [*TP, *AP, YP, AP[0]]
        y_T, lg_ps, rk_ps = ([v[:, a:a + 2 * w].rearrange("p (u e) -> p u e", e=w) for v in (YP, SC[0])]
                             for a, w in ((0, P), (256, E), (320, E)))
        ct_ps = SC[0][0:1, 384:384 + E]
        HP, DP = bank[4:6], bank[7]

        ld_x = [sem(f"ld_x{b}") for b in range(B)]
        ld_ctx, ld_wkv, ld_vec, ld_gate = sem("ld_ctx"), sem("ld_wkv"), sem("ld_vec"), sem("ld_gate")
        ld_wq, ld_wo, ld_f1, ld_f2, ld_gw = sem("ld_wq"), sem("ld_wo"), sem("ld_f1"), sem("ld_f2"), sem("ld_gw")
        ld_ws = [sem(f"ld_ws{n}") for n in range(len(STAGES))]
        ld_w2 = sem("ld_w2")
        regions_blank = sem("regions_blank")
        consts = sem("consts")
        cvar_ready, crs_ready, chat_ready = sem("cvar_ready"), sem("crs_ready"), sem("chat_ready")
        xvar_ready, xrs_ready = sem("xvar_ready"), sem("xrs_ready")
        cT_ready, cn_ready, kv_ready, kv_used = sem("cT_ready"), sem("cn_ready"), sem("kv_ready"), sem("kv_used")
        wqT_ready, wqT_used = sem("wqT_ready"), sem("wqT_used")
        a_ready, ahi_ready, a_used = sem("a_ready"), sem("ahi_ready"), sem("a_used")
        vo_ready, vo_used = sem("vo_ready"), sem("vo_used")
        f1hi_ready, f1_split = sem("f1hi_ready"), sem("f1_split")
        tg_ready = sem("tg_ready")
        xh_ready, xT_ready, xn_ready, xn_split = sem("xh_ready"), sem("xT_ready"), sem("xn_ready"), sem("xn_split")
        xn_hi_ready = sem("xn_hi_ready")
        ff_ready, ff_added = sem("ff_ready"), sem("ff_added")
        fg_ready, fu_ready, fsilu_ready, fh_ready = sem("fg_ready"), sem("fu_ready"), sem("fsilu_ready"), sem("fh_ready")
        zeros_ready = sem("zeros_ready")
        whi_ready, w_split = sem("whi_ready"), sem("w_split")
        scores_ready, nmax_ready, shift_ready, tail_ready, exp_ready = (
            sem("scores_ready"), sem("nmax_ready"), sem("shift_ready"), sem("tail_ready"), sem("exp_ready"))
        rsum_ready, probs_ready, last_probs_ready = sem("rsum_ready"), sem("probs_ready"), sem("last_probs_ready")
        tp_ready, tp_copied, acc_ready = sem("tp_ready"), sem("tp_copied"), sem("acc_ready")
        var2_ready, r2_ready, y_ready = sem("var2_ready"), sem("r2_ready"), sem("y_ready")
        yT_ready, yT_copied, row_copied = sem("yT_ready"), sem("yT_copied"), sem("row_copied")
        acc_read, before_ready = sem("acc_read"), sem("before_ready")
        logits_ready, ntop_ready, e2_ready = sem("logits_ready"), sem("ntop_ready"), sem("e2_ready")
        picks_ready, rank_ready, slots_ready = sem("picks_ready"), sem("rank_ready"), sem("slots_ready")
        rows_out = sem("rows_out")
        tables_ready = sem("tables_ready")
        rt_in = [sem(f"rt_in{k}") for k in range(RIN)]
        sT_ready, shi_ready, s_split = sem("sT_ready"), sem("shi_ready"), sem("s_split")
        sgate_ready, sup_ready, silu_ready, he_ready = sem("sgate_ready"), sem("sup_ready"), sem("silu_ready"), sem("he_ready")
        heT_ready, heT_copied = sem("heT_ready"), sem("heT_copied")
        ye_ready, yo_ready = sem("ye_ready"), sem("yo_ready")
        yo_out = [sem(f"yo_out{k}") for k in range(RIN)]
        back_in = [sem(f"back_in{n}") for n in range(len(QUARTERS))]
        osum_ready = [sem(f"osum_ready{n}") for n in range(len(QUARTERS))]
        out_done = sem("out_done")
        dve_steps = sem("dve_steps")
        pool_steps = sem("pool_steps")

        x_v = x.rearrange("b (t p) d -> p (b t) d", p=P)
        out_v = out.rearrange("b (t p) d -> p (b t) d", p=P)
        PAIR_TURNS = TILES // 2

        def from_(t, k):
            return not isinstance(t, int) or t >= k

        def heads_of(row, a, b):
            return row[:, a * J:b * J].rearrange("p (h j) -> p h j", j=J)

        def folds_after(j):
            down_at = FF // P
            return [] if j < 2 else [j - 2] if j < down_at else [j - 2, j - 1] if j == down_at else [j - 1]

        def is_last(i):
            return i == PAIR_TURNS - 1

        def has_own_rows(i):
            return i >= PAIR_TURNS - 2

        def rows_of(i):
            return last_rows[i % 2] if has_own_rows(i) else rows

        def slot_of(i):
            return last_slot[i % 2] if has_own_rows(i) else slot

        def reuses_rows(i):
            return from_(i, 1) and not has_own_rows(i)

        def slots_ahead(s, k):
            return not isinstance(s, int) or s + k < SLOT_TILES

        def slot_loop(engine, turn):
            for s in range(RIN):
                turn(s, s, s % 2)
            with engine.Fori(1, (SLOT_TILES - 2) // RIN) as i:
                for k in range(RIN):
                    turn(RIN * i + k, k, k % 2)
            for s in range((SLOT_TILES - 2) // RIN * RIN, SLOT_TILES):
                turn(s, s % RIN, s % 2)

        POOL_QUARTER = 1

        def add_returned(engine, ops, steps, n):
            ts = QUARTERS[n]
            engine.wait_ge(back_in[n], 16)
            steps.link(ops.tensor_tensor(X2[:, ts, :], X2[:, ts, :], back[:, ts, 0:D], ALU.add))
            ops.tensor_tensor(X2[:, ts, :], X2[:, ts, :], back[:, ts, D:2 * D], ALU.add).then_inc(osum_ready[n], 1)

        block = ctx.enter_context(nc.Block())

        @block.sync
        def _(sp):
            tiles_of = [slice(PER_BATCH * b, PER_BATCH * (b + 1)) for b in range(B)]
            sp.dma_start(X[:, tiles_of[0], :], x_v[:, tiles_of[0]]).then_inc(ld_x[0], 16)
            sp.dma_start(F1, wff1).then_inc(ld_f1, 16)
            sp.dma_start(X[:, tiles_of[1], :], x_v[:, tiles_of[1]]).then_inc(ld_x[1], 16)
            for n, v in enumerate((ln_g, ln_b, cln_g, cln_b)):
                sp.dma_start(lng[:, n:n + 1], v.rearrange("(p a) -> p a", a=1)).then_inc(ld_vec, 16)
            sp.dma_start(WQ, wq).then_inc(ld_wq, 16)
            wkv_v = wkv.rearrange("p (w d) -> p w d", w=2)
            for c in range(2):
                sp.dma_start(WKV2[:, :, c, :], wkv_v).then_inc(ld_wkv, 16)
            sp.dma_start(F2[:, :, :], wff2.rearrange("(q p) d -> p q d", p=P)).then_inc(ld_f2, 16)
            for n, (e0, e1, place) in enumerate(STAGES):
                sp.dma_start(place[:, :, 0:F], w1[e0:e1].rearrange("e d f -> d e f")).then_inc(ld_ws[n], 16)
                sp.dma_start(place[:, :, F:2 * F], w3[e0:e1].rearrange("e d f -> d e f")).then_inc(ld_ws[n], 16)
            sp.wait_ge(xT_ready, B)
            sp.dma_start(WO, wo.rearrange("(q p) d -> p q d", p=P)).then_inc(ld_wo, 16)
            sp.dma_start(GB[:, :], gate_b.partition_broadcast(P)).then_inc(ld_gw, 16)
            sp.dma_start(GW[:, :], gate_w).then_inc(ld_gw, 16)
            sp.wait_ge(consts, 1)
            half_r = REGION // P // 2 * P
            for r0, r1 in ((0, half_r), (half_r, REGION)):
                sp.dma_start(dispatched[r0:r1].rearrange("(t p) c -> p t c", p=P),
                             padrow[:, :].unsqueeze(1).to_broadcast([P, (r1 - r0) // P, ROW])).then_inc(regions_blank, 16)
            sp.wait_ge(w_split, STAGES[1][1])
            sp.dma_start(W2[:, :, :].rearrange("p e (q d) -> p e q d", d=D),
                         w2.rearrange("e (q p) d -> p e q d", p=P)).then_inc(ld_w2, 16)

            sp.wait_ge(w_split, E)
            sp.wait_ge(tables_ready, 1)

            def load_slots(s, k):
                row = sp.value_load(row_of[0:1, bass.ds(s, 1)], min_val=0, max_val=REGION - P)
                if isinstance(s, int) and s == 0:
                    sp.wait_ge(rows_out, 2 * TILES * 16)
                if from_(s, RIN):
                    sp.wait_ge(yo_out[k], (s // RIN) * 16)
                sp.dma_start(RT[:, k, :], dispatched[bass.ds(row, P), :]).then_inc(rt_in[k], 16)

            slot_loop(sp, lambda s, k, u: load_slots(s, k))

            for k in range(RIN):
                sp.wait_ge(yo_out[k], len(range(k, SLOT_TILES, RIN)) * 16)
            back_v = returned.rearrange("(t p k) d -> p t (k d)", p=P, k=2)
            for n, ts in enumerate(QUARTERS):
                sp.dma_start(back[:, ts], back_v[:, ts]).then_inc(back_in[n], 16)
            for n, ts in enumerate(QUARTERS):
                sp.wait_ge(osum_ready[n], 1)
                sp.dma_start(out_v[:, ts], X2[:, ts, :]).then_inc(out_done, 16)
            sp.wait_ge(out_done, len(QUARTERS) * 16)

        @block.gpsimd
        def _(gp):
            steps = Steps(gp, pool_steps)
            nc.gpsimd.memset(padrow[:, 0:D], 0.0)
            nc.gpsimd.memset(padrow[:, D + 1:ROW], 0.0)
            steps.link(nc.gpsimd.iota(padrow[:, D:D + 1].bitcast(U32), pattern=[[0, 1]], base=RETURN, channel_multiplier=0))
            nc.gpsimd.memset(half[:, :], -0.5).then_inc(consts, 1)
            steps.link(nc.gpsimd.memset(identf[:, :], 0.0))
            nc.gpsimd.affine_select(out=identf[:, :], in_=identf[:, :], compare_op=ALU.not_equal, fill=1.0,
                                    base=0, pattern=[[-1, P]], channel_multiplier=1).then_inc(consts, 1)
            nc.gpsimd.memset(kdiag[:, :, :, :], 0.0)
            nc.gpsimd.memset(vpad[:, :, :], 0.0).then_inc(zeros_ready, 1)

            def rsqrt_x(b):
                ts = slice(PER_BATCH * b, PER_BATCH * (b + 1))
                gp.wait_ge(xvar_ready, b + 1)
                nc.gpsimd.tensor_tensor(rx[:, ts], veps[:, ts], half[:, ts], ALU.pow).then_inc(xrs_ready, 1)

            rsqrt_x(0)
            gp.wait_ge(cvar_ready, 1)
            nc.gpsimd.tensor_tensor(rc[:, :], cveps[:, :], half[0:J, 0:B], ALU.pow).then_inc(crs_ready, 1)
            rsqrt_x(1)
            steps.link(nc.gpsimd.memset(ones_b[:, :], 1.0))
            nc.gpsimd.affine_select(out=lower_b[:, :], in_=ones_b[:, :], compare_op=ALU.is_gt, fill=0.0,
                                    base=0, pattern=[[1, P]], channel_multiplier=-1)
            nc.gpsimd.iota(iota_e[:, :], pattern=[[1, E]], base=0, channel_multiplier=0)
            nc.gpsimd.iota(before[:, :], pattern=[[CAP // P, E]], base=0, channel_multiplier=0,
                           allow_small_or_imprecise_dtypes=True)
            nc.gpsimd.iota(base_e[:, :], pattern=[[CAP, E]], base=0, channel_multiplier=0,
                           allow_small_or_imprecise_dtypes=True)
            nc.gpsimd.iota(iota_s[:, :], pattern=[[1, SLOT_TILES]], base=0, channel_multiplier=0,
                           allow_small_or_imprecise_dtypes=True)
            nc.gpsimd.iota(dest0[:, :, :], pattern=[[2 * P, 2], [1, 2]], base=0, channel_multiplier=2)
            nc.gpsimd.iota(pair_step[:, :, :], pattern=[[0, 2], [0, 2]], base=4 * P, channel_multiplier=0)
            steps.link(nc.gpsimd.memset(tri[:, :, :], 1.0))
            steps.link(nc.gpsimd.affine_select(out=tri[:, :, :], in_=tri[:, :, :], compare_op=ALU.is_ge, fill=0.0,
                                               base=0, pattern=[[1, E], [-1, E]], channel_multiplier=0))
            row_dest = rows[:, :, :, D:D + 1].bitcast(U32).rearrange("p t k a -> p t (k a)")
            nc.gpsimd.tensor_copy(row_dest, dest0[:, :, :]).then_inc(consts, 1)

            for e0, e1, place in STAGES:
                for e in range(e0, e1):
                    gp.wait_ge(whi_ready, e + 1)
                    nc.gpsimd.tensor_tensor(W13_lo[:, e, :], place[:, e - e0, :], W13_hi[:, e, :].bitcast(F32),
                                            ALU.subtract).then_inc(w_split, 1)

            def normalise(t, u):
                gp.wait_ge(rsum_ready, t + 1)
                h0 = SHARED if t == TILES - 1 else 0
                v = heads_of(PR[:, u, :], h0, H)
                nc.gpsimd.tensor_tensor(v, v, RI[:, u, h0:H].unsqueeze(2).to_broadcast([P, H - h0, J]),
                                        ALU.mult).then_inc(probs_ready, 1)

            def rsqrt2(i, tiles=(0, 1)):
                gp.wait_ge(var2_ready, 2 * i + tiles[-1] + 1)
                ns = slice(tiles[0], tiles[-1] + 1)
                nc.gpsimd.tensor_tensor(r2[:, ns], ve2[:, ns], half[:, ns], ALU.pow).then_inc(r2_ready, len(tiles))

            def dispatch(i, n):
                if n == 0:
                    gp.wait_ge(slots_ready, i + 1)
                    gp.wait_ge(row_copied, i + 1)
                    if reuses_rows(i):
                        gp.wait_ge(rows_out, i * 64)
                        steps.did(nc.gpsimd.tensor_tensor(row_dest, row_dest, pair_step[:, :, :], ALU.add))
                    steps.wait()
                    gp.wait_ge(regions_blank, 32)
                for k in range(2):
                    gp.indirect_dma_start(dispatched[:, :], bass.IndirectOffsetOnAxis(slot_of(i)[:, n, k:k + 1], 0),
                                          rows_of(i)[:, n, k, :], None).then_inc(rows_out, 16)

            gp.wait_ge(ff_ready, B)
            for i in range(PAIR_TURNS - 2, PAIR_TURNS):
                steps.did(nc.gpsimd.iota(rows_of(i)[:, :, :, D:D + 1].bitcast(U32).rearrange("p t k a -> p t (k a)"),
                                         pattern=[[2 * P, 2], [1, 2]], base=i * 4 * P, channel_multiplier=2))

            for i in range(PAIR_TURNS):
                if i >= 2:
                    rsqrt2(i - 2)
                if i >= 3:
                    dispatch(i - 3, 0)
                if i >= 1:
                    normalise(2 * i - 1, 1)
                if i >= 3:
                    dispatch(i - 3, 1)
                normalise(2 * i, 0)
            rsqrt2(PAIR_TURNS - 2)
            normalise(TILES - 1, 1)
            dispatch(PAIR_TURNS - 3, 0)
            rsqrt2(PAIR_TURNS - 1, (0,))
            dispatch(PAIR_TURNS - 3, 1)
            rsqrt2(PAIR_TURNS - 1, (1,))
            dispatch(PAIR_TURNS - 2, 0)
            dispatch(PAIR_TURNS - 2, 1)
            for n in range(2):
                dispatch(PAIR_TURNS - 1, n)

            for s in range(SLOT_TILES):
                k = s % RIN
                gp.wait_ge(yo_ready, s + 1)
                gp.indirect_dma_start(returned[:, :], bass.IndirectOffsetOnAxis(RT[:, k, D:D + 1].bitcast(U32), 0),
                                      YO[:, k, :], None, bounds_check=RETURN - 1,
                                      oob_is_err=False).then_inc(yo_out[k], 16)

            add_returned(gp, nc.gpsimd, steps, POOL_QUARTER)

        @block.scalar
        def _(act):
            act.dma_start(CTX[:, :, :], ctx_in.rearrange("b j d -> j b d")).then_inc(ld_ctx, 16)
            for n, v in enumerate((g_xattn, g_ffn)):
                act.dma_start(gates[:, n:n + 1], v.partition_broadcast(P)).then_inc(ld_gate, 16)

            act.wait_ge(ld_gate, 32)
            nc.scalar.activation(tg[:, :], gates[:, :], ACT.Tanh).then_inc(tg_ready, 1)
            act.wait_ge(ld_f1, 16)
            nc.scalar.activation(F1_hi[:, :], F1, ACT.Copy).then_inc(f1hi_ready, 1)
            act.wait_ge(ld_vec, 64)

            def affine_xn(b):
                act.wait_ge(xT_ready, b + 1)
                nc.scalar.activation(XN[:, b, :], XP[:, :], ACT.Identity, bias=lng[:, 1:2],
                                     scale=lng[:, 0:1]).then_inc(xn_ready, 1)

            def a_hi(p):
                act.wait_ge(a_ready, p + 1)
                nc.scalar.activation(A_hi[:, :, 2 * J * p:2 * J * (p + 1)],
                                     A_PS[p % 2][:, 0:B * 2 * J].rearrange("p (b c) -> p b c", b=B),
                                     ACT.Copy).then_inc(ahi_ready, 1)

            def expert_hi(e):
                n, (e0, _, place) = next((n, st) for n, st in enumerate(STAGES) if st[0] <= e < st[1])
                act.wait_ge(ld_ws[n], 32)
                nc.scalar.activation(W13_hi[:, e, :], place[:, e - e0, :], ACT.Copy).then_inc(whi_ready, 1)

            affine_xn(0)
            for j in range(B * (FF // P)):
                act.wait_ge(fg_ready, j + 1)
                if j >= 2:
                    act.wait_ge(fh_ready, j - 1)
                nc.scalar.activation(SG[:, j % 2, :], GP[j % 2][:, :], ACT.Silu).then_inc(fsilu_ready, 1)
                if j == 0:
                    act.wait_ge(cT_ready, 1)
                    nc.scalar.activation(CN[:, :], CP[:, 0:B * J], ACT.Identity, bias=lng[:, 3:4],
                                         scale=lng[:, 2:3]).then_inc(cn_ready, 1)
                    for g in range(2):
                        act.wait_ge(wqT_ready, g + 1)
                        nc.scalar.activation(WQT[:, 4 * g:4 * g + 4, :].rearrange("p q d -> p (q d)"), QP[g][:, :],
                                             ACT.Copy).then_inc(wqT_used, 1)
                elif j == 1:
                    affine_xn(1)
                for p in folds_after(j)[0:1]:
                    a_hi(p)
                if j == B * (FF // P) - 1:
                    a_hi(PAIRS - 1)
                if j >= 1:
                    expert_hi(j - 1)
                for p in folds_after(j)[1:]:
                    a_hi(p)

            def exp_tail(t, u, i=None):
                act.wait_ge(nmax_ready, t + 1)
                if from_(t, 2):
                    act.wait_ge(tp_ready, 3 * (t - 1))
                for h in range(TAIL, H):
                    if i is not None and h == TAIL + 2:
                        pass_yT(i)
                    last = nc.scalar.activation(PR[:, u, h * J:(h + 1) * J], SC[2][:, (h - TAIL) * J:(h - TAIL + 1) * J],
                                                ACT.Exp, bias=nM[:, u, h:h + 1], accum_out=RS[:, u, h:h + 1])
                last.then_inc(tail_ready, 1)

            def exp_shifted(t, u):
                act.wait_ge(shift_ready, t + 1)
                v = PR[:, u, 0:TAIL * J]
                nc.scalar.activation(v, v, ACT.Exp).then_inc(exp_ready, 1)

            def copy_probs(t, i=None):
                for q in range(3):
                    if i is not None and q == 2:
                        pass_yT(i)
                    act.wait_ge(tp_ready, 3 * t + q + 1)
                    if from_(t, 1):
                        act.wait_ge(acc_ready, t)
                    tp, (a, e) = TP[q % 2], GROUPS[q]
                    full = min(e, CH - 1)
                    last = nc.scalar.activation(PT[:, a:full, :].rearrange("p q d -> p (q d)"), tp[:, 0:(full - a) * P],
                                                ACT.Copy)
                    if e == CH:
                        last = nc.scalar.activation(PT[0:LASTC, full, :], tp[0:LASTC, (full - a) * P:(e - a) * P],
                                                    ACT.Copy)
                    last.then_inc(tp_copied, 1)

            def pass_yT(i):
                act.wait_ge(yT_ready, i + 1)
                nc.scalar.activation(YT[:, :, :], y_T[is_last(i)], ACT.Copy).then_inc(yT_copied, 1)

            def pass_rows(i):
                act.wait_ge(y_ready, 2 * i + 2)
                if reuses_rows(i):
                    act.wait_ge(rows_out, i * 64)
                for k in range(2):
                    last = nc.scalar.activation(rows_of(i)[:, :, k, 0:D], YB[:, :, :], ACT.Copy)
                last.then_inc(row_copied, 1)

            def weigh_choices(i):
                act.wait_ge(ntop_ready, i + 1)
                if from_(i, 1):
                    act.wait_ge(slots_ready, i)
                for n in range(2):
                    last = nc.scalar.activation(e2[:, n, :], MX[:, n, 0:2], ACT.Exp, bias=ntop[:, n:n + 1],
                                                accum_out=esum[:, n:n + 1])
                last.then_inc(e2_ready, 1)

            def pair_turn(i):
                copy_probs(2 * i - 2)
                exp_tail(2 * i, 0, i - 2 if from_(i, 2) else None)
                exp_shifted(2 * i, 0)
                if from_(i, 2):
                    weigh_choices(i - 2)
                copy_probs(2 * i - 1)
                exp_tail(2 * i + 1, 1)
                exp_shifted(2 * i + 1, 1)
                if from_(i, 2):
                    pass_rows(i - 2)

            exp_tail(0, 0)
            exp_shifted(0, 0)
            expert_hi(E - 1)
            exp_tail(1, 1)
            exp_shifted(1, 1)
            for i in range(1, PAIR_TURNS):
                pair_turn(i)
            copy_probs(TILES - 2)
            copy_probs(TILES - 1, PAIR_TURNS - 2)
            pass_rows(PAIR_TURNS - 2)
            weigh_choices(PAIR_TURNS - 2)
            pass_yT(PAIR_TURNS - 1)
            pass_rows(PAIR_TURNS - 1)
            weigh_choices(PAIR_TURNS - 1)
            nc.scalar.activation(SG[:, 0, 0:1], tg[:, 0:1], ACT.Silu)

            def slot_hi(s, u):
                act.wait_ge(sT_ready, s + 1)
                if from_(s, 2):
                    act.wait_ge(sup_ready, s - 1)
                nc.scalar.activation(XT_hi[u][:, :], XP[:, 0:P], ACT.Copy).then_inc(shi_ready, 1)

            def silu(s, u):
                act.wait_ge(sgate_ready, s + 1)
                if from_(s, 2):
                    act.wait_ge(he_ready, 2 * (s - 1))
                nc.scalar.activation(SG[:, u, :], GP[u][:, :], ACT.Silu).then_inc(silu_ready, 1)

            def slot_turn(s, k, u):
                act.wait_ge(heT_ready, s + 1)
                if from_(s, 2):
                    act.wait_ge(ye_ready, s - 1)
                nc.scalar.activation(HT[:, u, :, :].rearrange("p q d -> p (q d)"), HP[u][:, :],
                                     ACT.Copy).then_inc(heT_copied, 1)
                if slots_ahead(s, 1):
                    silu(s + 1, 1 - u)
                if slots_ahead(s, 2):
                    slot_hi(s + 2, u)
                act.wait_ge(ye_ready, s + 1)
                if from_(s, RIN):
                    act.wait_ge(yo_out[k], s // RIN * 16)
                nc.scalar.activation(YO[:, k, :], DP[:, 0:D], ACT.Copy,
                                     scale=RT[:, k, D + 1:D + 2]).then_inc(yo_ready, 1)

            slot_hi(0, 0)
            silu(0, 0)
            slot_hi(1, 1)
            slot_loop(act, slot_turn)

        @block.vector
        def _(dve):
            steps = Steps(dve, dve_steps)
            def statistics_x(b):
                dve.wait_ge(ld_x[b], 16)
                ts = slice(PER_BATCH * b, PER_BATCH * (b + 1))
                for t in range(ts.start, ts.stop):
                    last = nc.vector.bn_stats(stats[:, t, :], X[:, t, :])
                steps.link(last)
                for t in range(ts.start, ts.stop):
                    last = nc.vector.bn_aggr(mv[:, t, :], stats[:, t, :])
                steps.link(last)
                nc.vector.tensor_scalar(veps[:, ts], mv[:, ts, 1], 1.0 + EPS, EPS * EPS, ALU.mult,
                                        ALU.add).then_inc(xvar_ready, 1)

            statistics_x(0)
            dve.wait_ge(ld_ctx, 16)
            for b in range(B):
                last = nc.vector.bn_stats(cstats[:, b, :], CTX[:, b, :])
            steps.link(last)
            for b in range(B):
                last = nc.vector.bn_aggr(cmv[:, b, :], cstats[:, b, :])
            steps.link(last)
            nc.vector.tensor_scalar(cveps[:, :], cmv[:, :, 1], EPS, None, ALU.add).then_inc(cvar_ready, 1)

            def xhat(b):
                dve.wait_ge(xrs_ready, b + 1)
                for t in range(PER_BATCH * b, PER_BATCH * (b + 1)):
                    last = nc.vector.tensor_scalar(X2[:, t, :], X[:, t, :], mv[:, t, 0:1], rx[:, t:t + 1], ALU.subtract,
                                                   ALU.mult)
                last.then_inc(xh_ready, 1)

            def split_xn(b):
                dve.wait_ge(xn_ready, b + 1)
                ts = slice(PER_BATCH * b, PER_BATCH * (b + 1))
                hi, lo = (v[:, ts, :].rearrange("p t c -> p (t c)") for v in (xnT_hi, xnT_lo))
                nc.vector.tensor_copy(hi, XN[:, b, :]).then_inc(xn_hi_ready, 1)
                dve.wait_ge(xn_hi_ready, b + 1)
                nc.vector.tensor_tensor(lo, XN[:, b, :], hi.bitcast(F32), ALU.subtract).then_inc(xn_split, 1)

            xhat(0)
            dve.wait_ge(f1hi_ready, 1)
            nc.vector.tensor_tensor(F1_lo[:, :], F1, F1_hi[:, :].bitcast(F32), ALU.subtract).then_inc(f1_split, 1)
            dve.wait_ge(crs_ready, 1)
            for b in range(B):
                nc.vector.tensor_scalar(CHAT[:, b, :], CTX[:, b, :], cmv[:, b, 0:1], rc[:, b:b + 1], ALU.subtract,
                                        ALU.mult).then_inc(chat_ready, 1)
            split_xn(0)
            statistics_x(1)

            def place_keys_values():
                dve.wait_ge(zeros_ready, 1)
                dve.wait_ge(kv_ready, 1)
                kv = CP[:, 0:2 * B * J].rearrange("p (w b j) -> p w b j", w=2, b=B)
                for c in range(2):
                    rws = slice(DH * c, DH * (c + 1))
                    nc.vector.tensor_scalar(kdiag[rws, :, c, :], kv[rws, 0], DH ** -0.5, None, ALU.mult)
                    last = nc.vector.tensor_copy(vpad[rws, :, P + J * c:P + J * (c + 1)], kv[rws, 1])
                last.then_inc(kv_used, 1)
            dve.wait_ge(tg_ready, 1)

            def add_ff(b):
                dve.wait_ge(ff_ready, b + 1)
                xb = X[:, PER_BATCH * b:PER_BATCH * (b + 1), :].rearrange("p t d -> p (t d)")
                nc.vector.scalar_tensor_tensor(xb, FP[:, :], tg[:, 0:1], xb, ALU.mult, ALU.add).then_inc(ff_added, 1)

            def a_lo(p):
                dve.wait_ge(ahi_ready, p + 1)
                cs = slice(2 * J * p, 2 * J * (p + 1))
                nc.vector.tensor_tensor(A_lo[:, :, cs], A_PS[p % 2][:, 0:B * 2 * J].rearrange("p (b c) -> p b c", b=B),
                                        A_hi[:, :, cs].bitcast(F32), ALU.subtract).then_inc(a_used, 1)

            for j in range(B * (FF // P)):
                b, c = divmod(j, FF // P)
                if b > 0 and c == 0:
                    add_ff(b - 1)
                dve.wait_ge(fsilu_ready, j + 1)
                dve.wait_ge(fu_ready, j + 1)
                nc.vector.tensor_tensor(HC[:, c, :], SG[:, j % 2, :], UP[j % 2][:, :], ALU.mult).then_inc(fh_ready, 1)
                if j == 0:
                    xhat(1)
                    place_keys_values()
                elif j == 1:
                    split_xn(1)
                for p in folds_after(j):
                    a_lo(p)
            a_lo(PAIRS - 1)

            S4 = [SC[g][:, 0:(e - a) * J].rearrange("p (h j) -> p h j", j=J) for g, (a, e) in enumerate(HEADS)]

            def maxima(t, u):
                for g, (a, b) in enumerate(HEADS):
                    dve.wait_ge(scores_ready, 3 * t + g + 1)
                    last = nc.vector.tensor_reduce(nM[:, u, a:b], S4[g], AX_X, ALU.max, negate=True)
                last.then_inc(nmax_ready, 1)

            def shift(t, u):
                dve.wait_ge(nmax_ready, t + 1)
                if from_(t, 2):
                    dve.wait_ge(tp_ready, 3 * (t - 1))
                for g in range(2):
                    a, b = HEADS[g]
                    last = nc.vector.tensor_tensor(PR[:, u, a * J:b * J].rearrange("p (h j) -> p h j", j=J), S4[g],
                                                   nM[:, u, a:b].unsqueeze(2).to_broadcast([P, b - a, J]), ALU.add)
                last.then_inc(shift_ready, 1)

            def sums(t, u):
                dve.wait_ge(exp_ready, t + 1)
                steps.link(nc.vector.tensor_reduce(RS[:, u, 0:TAIL], PR[:, u, 0:TAIL * J].rearrange("p (h j) -> p h j", j=J),
                                                   AX_X, ALU.add))
                nc.vector.reciprocal(RI[:, u, :], RS[:, u, :]).then_inc(rsum_ready, 1)

            def residual(t, u):
                dve.wait_ge(acc_ready, t + 1)
                nc.vector.scalar_tensor_tensor(X2[:, t, :], AP[u][:, 0:D], tg[:, 0:1], X[:, t, :], ALU.mult,
                                               ALU.add).then_inc(acc_read, 1)

            def variance(i, tiles=(0, 1)):
                dve.drain()
                for n in tiles:
                    nc.vector.bn_stats(st2[:, n, :], X2[:, 2 * i + n, :])
                dve.drain()
                for n in tiles:
                    last = nc.vector.bn_aggr(mv2[:, n, :], st2[:, n, :])
                steps.link(last)
                ns = slice(tiles[0], tiles[-1] + 1)
                nc.vector.tensor_scalar(ve2[:, ns], mv2[:, ns, 1], EPS, None, ALU.add).then_inc(var2_ready, len(tiles))

            def normed(i, tiles=(0, 1)):
                dve.wait_ge(r2_ready, 2 * i + tiles[-1] + 1)
                if from_(i, 1) and 0 in tiles:
                    dve.wait_ge(row_copied, i)
                for n in tiles:
                    last = nc.vector.tensor_scalar(YB[:, n, :], X2[:, 2 * i + n, :],
                                                   mv2[:, n, 0:1], r2[:, n:n + 1], ALU.subtract, ALU.mult)
                last.then_inc(y_ready, len(tiles))

            def choose(i):
                dve.wait_ge(logits_ready, i + 1)
                nc.vector.tensor_tensor(LG[:, :, :], lg_ps[is_last(i)], GB[:, :].unsqueeze(1).to_broadcast([P, 2, E]), ALU.add)
                dve.drain()
                for n in range(2):
                    last = nc.vector.max(MX[:, n, :], LG[:, n, :])
                steps.link(last)
                nc.vector.tensor_scalar(ntop[:, :], MX[:, :, 0], -1.0, None, ALU.mult).then_inc(ntop_ready, 1)
                for n in range(2):
                    last = nc.vector.max_index(IX[:, n, :], MX[:, n, :], LG[:, n, :])
                steps.link(last)
                iota4 = iota_e[:, :].unsqueeze(1).to_broadcast([P, 2, E]).unsqueeze(1).to_broadcast([P, 2, 2, E])
                nc.vector.tensor_tensor(pick[:, :, :, :], iota4, IX[:, :, 0:2].unsqueeze(3).to_broadcast([P, 2, 2, E]),
                                        ALU.is_equal).then_inc(picks_ready, 1)

            def place(i):
                dve.wait_ge(e2_ready, i + 1)
                steps.link(nc.vector.reciprocal(esinv[:, :], esum[:, :]))
                if reuses_rows(i):
                    dve.wait_ge(rows_out, i * 64)
                nc.vector.scalar_tensor_tensor(rows_of(i)[:, :, :, D + 1:D + 2].rearrange("p t k a -> p t (k a)"), e2[:, :, :],
                                               tg[:, 1:2], esinv[:, :].unsqueeze(2).to_broadcast([P, 2, 2]), ALU.mult,
                                               ALU.mult)
                dve.wait_ge(rank_ready, i + 1)
                steps.link(nc.vector.tensor_tensor(prod[:, :, :, :], pick[:, :, :, :],
                                                   rk_ps[is_last(i)].unsqueeze(2).to_broadcast([P, 2, 2, E]), ALU.mult))
                with nc.allow_low_precision("slot numbers are whole numbers below 2^24"):
                    nc.vector.tensor_reduce(slot_of(i)[:, :, :], prod[:, :, :, :], AX_X, ALU.add).then_inc(slots_ready, 1)

            def count_choices():
                with nc.allow_low_precision("counts are whole numbers up to 2 * TILES + CAP / P * E, exact in bf16"):
                    steps.link(nc.vector.tensor_reduce(picked[:, :], pick[:, :, :, :].rearrange("p t k e -> p e t k"),
                                                       mybir.AxisListType.XY, ALU.add))
                    nc.vector.tensor_tensor(before[:, :], before[:, :], picked[:, :], ALU.add).then_inc(before_ready, 1)

            def pair_turn(i, begun=False):
                if from_(i, 2):
                    residual(2 * i - 3, 1)
                    variance(i - 2)
                if not begun:
                    maxima(2 * i, 0)
                if from_(i, 2):
                    normed(i - 2)
                if not begun:
                    sums(2 * i - 1, 1)
                shift(2 * i, 0)
                if from_(i, 2):
                    choose(i - 2)
                residual(2 * i - 2, 0)
                maxima(2 * i + 1, 1)
                sums(2 * i, 0)
                shift(2 * i + 1, 1)
                if from_(i, 2):
                    place(i - 2)
                    count_choices()

            maxima(0, 0)
            shift(0, 0)
            add_ff(B - 1)

            def copy_vo(g):
                if g == 0:
                    dve.wait_ge(w_split, E)
                dve.wait_ge(vo_ready, g + 1)
                b, c = divmod(g, 3)
                n = min(4, CH - 4 * c)
                nc.vector.tensor_copy(VO[:, b, 4 * c:4 * c + n, :].rearrange("p q d -> p (q d)"),
                                      VO_PS[g][:, 0:n * P]).then_inc(vo_used, 1)

            sums(0, 0)
            maxima(1, 1)
            shift(1, 1)
            for g in range(3):
                copy_vo(g)
            maxima(2, 0)
            sums(1, 1)
            for g in range(3, 6):
                copy_vo(g)
            dve.wait_ge(ld_gw, 32)
            dve.wait_ge(consts, 3)
            for i in range(1, PAIR_TURNS):
                pair_turn(i, begun=i == 1)
            residual(TILES - 3, 1)
            variance(PAIR_TURNS - 2)
            sums(TILES - 1, 1)
            dve.wait_ge(rsum_ready, TILES)
            v = heads_of(PR[:, 1, :], 0, SHARED)
            nc.vector.tensor_tensor(v, v, RI[:, 1, 0:SHARED].unsqueeze(2).to_broadcast([P, SHARED, J]),
                                    ALU.mult).then_inc(last_probs_ready, 1)
            normed(PAIR_TURNS - 2)
            residual(TILES - 2, 0)
            variance(PAIR_TURNS - 1, (0,))
            choose(PAIR_TURNS - 2)
            normed(PAIR_TURNS - 1, (0,))
            residual(TILES - 1, 1)
            variance(PAIR_TURNS - 1, (1,))
            place(PAIR_TURNS - 2)
            count_choices()
            normed(PAIR_TURNS - 1, (1,))
            choose(PAIR_TURNS - 1)
            place(PAIR_TURNS - 1)

            with nc.allow_low_precision("counts are whole numbers below 2^24"):
                steps.link(nc.vector.scalar_tensor_tensor(T8u[:, :], ct_ps, float(P - 1), base_e[:, :], ALU.add,
                                                          ALU.subtract))
                steps.link(nc.vector.tensor_scalar(T8u[:, :], T8u[:, :], 7, None, ALU.logical_shift_right))
                steps.link(nc.vector.tensor_copy(Tn[:, :], T8u[:, :]))
                steps.link(nc.vector.tensor_tensor(TT[:, :, :], tri[:, :, :], Tn[:, :].unsqueeze(1).to_broadcast([1, E, E]), ALU.mult))
                steps.link(nc.vector.tensor_reduce(Tend[:, :], TT[:, :, :], AX_X, ALU.add))
                steps.link(nc.vector.tensor_tensor(GE[:, :, :], iota_s[:, :].unsqueeze(2).to_broadcast([1, SLOT_TILES, E]),
                                                   Tend[:, :].unsqueeze(1).to_broadcast([1, SLOT_TILES, E]), ALU.is_ge))
                steps.link(nc.vector.tensor_reduce(es[:, :], GE[:, :, :], AX_X, ALU.add))
                steps.link(nc.vector.tensor_tensor(GT[:, :, :], GE[:, :, :], Tn[:, :].unsqueeze(1).to_broadcast([1, SLOT_TILES, E]), ALU.mult))
                steps.link(nc.vector.tensor_reduce(ts_[:, :], GT[:, :, :], AX_X, ALU.add))
                steps.link(nc.vector.tensor_tensor(rowb[:, :], iota_s[:, :], ts_[:, :], ALU.subtract))
                steps.link(nc.vector.tensor_scalar(rowb[:, :], rowb[:, :], float(P), None, ALU.mult))
                nc.vector.tensor_scalar(expert_of[:, :], es[:, :], float(E - 1), None, ALU.min)
                nc.vector.scalar_tensor_tensor(row_of[:, :], es[:, :], float(CAP), rowb[:, :], ALU.mult,
                                               ALU.add).then_inc(tables_ready, 1)

            def slot_lo(s, u):
                dve.wait_ge(shi_ready, s + 1)
                nc.vector.tensor_tensor(XT_lo[u][:, :], XP[:, 0:P], XT_hi[u][:, :].bitcast(F32),
                                        ALU.subtract).then_inc(s_split, 1)

            def gate_up(s, u):
                dve.wait_ge(silu_ready, s + 1)
                dve.wait_ge(sup_ready, s + 1)
                if from_(s, 2):
                    dve.wait_ge(heT_ready, s - 1)
                for n in range(2):
                    cs = slice(n * F // 2, (n + 1) * F // 2)
                    nc.vector.tensor_tensor(HH[:, u, cs], SG[:, u, cs], UP[u][:, cs], ALU.mult).then_inc(he_ready, 1)

            def slot_turn(s, k, u):
                if slots_ahead(s, 1):
                    gate_up(s + 1, 1 - u)
                if slots_ahead(s, 2):
                    slot_lo(s + 2, u)

            slot_lo(0, 0)
            gate_up(0, 0)
            slot_lo(1, 1)
            slot_loop(dve, slot_turn)

            for n in range(len(QUARTERS)):
                if n != POOL_QUARTER:
                    add_returned(dve, nc.vector, steps, n)

        @block.tensor
        def _(pe):
            def mm3(o, l_hi, l_lo, r_hi, r_lo, before_r_lo=lambda: None):
                nc.tensor.matmul(o, l_hi, r_hi, start=True, stop=False)
                nc.tensor.matmul(o, l_lo, r_hi, start=False, stop=False)
                before_r_lo()
                return nc.tensor.matmul(o, l_hi, r_lo, start=False, stop=True)

            def keep_clock(products):
                for _ in range(products):
                    nc.tensor.matmul(bank[0][:, 0:P], identf[:, :], identf[:, :], start=True, stop=True)

            pe.wait_ge(consts, 2)
            keep_clock(12)

            def transpose_xhat(b):
                pe.wait_ge(xh_ready, b + 1)
                if b >= 1:
                    pe.wait_ge(xn_ready, b)
                for n in range(PER_BATCH):
                    last = nc.tensor.transpose(XP[:, n * P:(n + 1) * P], X2[:, PER_BATCH * b + n, :], identf[:, :])
                last.then_inc(xT_ready, 1)

            def transpose_context():
                pe.wait_ge(chat_ready, B)
                for b in range(B):
                    last = nc.tensor.transpose(CP[:, b * J:(b + 1) * J], CHAT[:, b, :], identf[0:J, 0:J])
                last.then_inc(cT_ready, 1)

            def transpose_wq():
                pe.wait_ge(ld_wq, 16)
                for g in range(2):
                    for q in range(4):
                        last = nc.tensor.transpose(QP[g][:, q * P:(q + 1) * P],
                                                   WQ[:, (4 * g + q) * P:(4 * g + q + 1) * P], identf[:, :])
                    last.then_inc(wqT_ready, 1)

            def keys_values():
                pe.wait_ge(ld_wkv, 32)
                pe.wait_ge(cn_ready, 1)
                for w in range(2):
                    last = nc.tensor.matmul(CP[:, w * B * J:(w + 1) * B * J],
                                            WKV2[:, w, :, :].rearrange("p c d -> p (c d)"), CN[:, :], start=True, stop=True)
                last.then_inc(kv_ready, 1)

            def gate_up(j):
                b, c = divmod(j, FF // P)
                pe.wait_ge(xn_hi_ready, b + 1)
                if j >= 2:
                    pe.wait_ge(fh_ready, j - 1)
                ts = slice(PER_BATCH * b, PER_BATCH * (b + 1))
                hi, lo = (v[:, ts, :].rearrange("p t c -> p (t c)") for v in (xnT_hi, xnT_lo))
                for o, c0, done in ((GP, FF, fg_ready), (UP, 0, fu_ready)):
                    cs = slice(c0 + c * P, c0 + (c + 1) * P)
                    mm3(o[j % 2][:, :], F1_hi[:, cs], F1_lo[:, cs], hi, lo,
                        before_r_lo=lambda: pe.wait_ge(xn_split, b + 1)).then_inc(done, 1)

            def fold_keys(p):
                if p >= 2:
                    pe.wait_ge(a_used, p - 1)
                nc.tensor.matmul(A_PS[p % 2][:, 0:B * 2 * J], WQT[:, p, :], kdiag[:, :, :, :].rearrange("p b c j -> p (b c j)"),
                                 start=True, stop=True).then_inc(a_ready, 1)

            def down(b):
                pe.wait_ge(fh_ready, (b + 1) * (FF // P))
                if b >= 1:
                    pe.wait_ge(ff_added, b)
                for n in range(PER_BATCH):
                    for c in range(FF // P):
                        last = nc.tensor.matmul(FP[:, n * P:(n + 1) * P], HC[:, c, n * P:(n + 1) * P], F2[:, c, :],
                                                start=c == 0, stop=c == FF // P - 1)
                last.then_inc(ff_ready, 1)

            transpose_xhat(0)
            pe.wait_ge(f1_split, 1)
            gate_up(0)
            transpose_context()
            transpose_wq()
            gate_up(1)
            keys_values()
            transpose_xhat(1)
            gate_up(2)
            pe.wait_ge(wqT_used, 2)
            pe.wait_ge(kv_used, 1)
            fold_keys(0)
            pe.wait_ge(ld_f2, 16)
            for j in range(3, B * (FF // P)):
                gate_up(j)
                for n, p in enumerate(folds_after(j)):
                    if n == 1:
                        down(0)
                    fold_keys(p)
            fold_keys(PAIRS - 1)

            def scores(t, b):
                pe.wait_ge(xn_split, B)
                for g, (a, e) in enumerate(HEADS):
                    if from_(t, 1):
                        if g == 0:
                            pe.wait_ge(shift_ready, t)
                        if g == 2:
                            pe.wait_ge(tail_ready, t)
                    elif g == 2:
                        pe.wait_ge(a_used, PAIRS)
                    n = (e - a) * J
                    hi = A_hi[:, b, a * J:e * J]
                    lo = A_lo[:, b, a * J:e * J]
                    mm3(SC[g][:, 0:n], xnT_hi[:, t, :], xnT_lo[:, t, :], hi, lo).then_inc(scores_ready, 1)

            def attend(t, u, b, i=None):
                last_tile = t == TILES - 1
                for q in range(3):
                    if q == 0:
                        pe.wait_ge(probs_ready, t + 1)
                        if last_tile:
                            pe.wait_ge(last_probs_ready, 1)
                    if q < 2:
                        if t == 0:
                            pe.wait_ge(vo_used, q + 1)
                        else:
                            pe.wait_ge(tp_copied, 3 * t)
                    else:
                        pe.wait_ge(tp_copied, 3 * t + 1)
                    for n, c in enumerate(range(*GROUPS[q])):
                        s = PR[:, u, c * P:min((c + 1) * P, HJ)]
                        w = s.shape[1]
                        last = nc.tensor.transpose(TP[q % 2][0:w, n * P:(n + 1) * P], s, identf[:, :])
                    last.then_inc(tp_ready, 1)
                    if last_tile and q == 1:
                        transpose_y(i)
                for q in range(3):
                    if i is not None and not last_tile and q == 2:
                        logits(i)
                    pe.wait_ge(tp_copied, 3 * t + q + 1)
                    if t == 0 and q == 0:
                        pe.wait_ge(vo_used, 6)
                    if q == 0 and from_(t, 2):
                        pe.wait_ge(acc_read, t - 1)
                    for c in range(*GROUPS[q]):
                        k = LASTC if c == CH - 1 else P
                        last = nc.tensor.matmul(AP[u][:, 0:D], PT[0:k, c, :],
                                                VO[0:k, b, c, :],
                                                start=c == 0, stop=c == CH - 1)
                    if i is not None and q == 0:
                        if last_tile:
                            logits(i)
                        else:
                            transpose_y(i)
                last.then_inc(acc_ready, 1)

            def transpose_y(i):
                pe.wait_ge(y_ready, 2 * i + 2)
                if from_(i, 1) and not is_last(i):
                    pe.wait_ge(slots_ready, i)
                for n in range(2):
                    last = nc.tensor.transpose(y_T[is_last(i)][:, n, :], YB[:, n, :], identf[:, :])
                last.then_inc(yT_ready, 1)

            def logits(i):
                pe.wait_ge(yT_copied, i + 1)
                for n in range(2):
                    last = nc.tensor.matmul(lg_ps[is_last(i)][:, n, :], YT[:, n, :], GW[:, :], start=True, stop=True)
                last.then_inc(logits_ready, 1)

            def ranks(i):
                pe.wait_ge(picks_ready, i + 1)
                if from_(i, 1):
                    pe.wait_ge(before_ready, i)
                if is_last(i):
                    for n in range(2):
                        for k in range(2):
                            nc.tensor.matmul(ct_ps, ones_b[:, 0:1], pick[:, n, k, :], start=(n, k) == (0, 0), stop=False)
                    nc.tensor.matmul(ct_ps, ones_b[:, 0:1], before[:, :], start=False, stop=True)
                rk = rk_ps[is_last(i)]
                for n in range(2):
                    for k in range(2):
                        nc.tensor.matmul(rk[:, n, :], lower_b[:, :], pick[:, n, k, :], start=k == 0, stop=False)
                        if n == 1:
                            nc.tensor.matmul(rk[:, n, :], ones_b[:, :], pick[:, 0, k, :], start=False, stop=False)
                    last = nc.tensor.matmul(rk[:, n, :], ones_b[:, :], before[:, :], start=False, stop=True)
                last.then_inc(rank_ready, 1)

            def pair_turn(i, begun=False):
                if not begun:
                    scores(2 * i, 2 * i // PER_BATCH)
                attend(2 * i - 2, 0, (2 * i - 2) // PER_BATCH, i - 2 if from_(i, 2) else None)
                scores(2 * i + 1, 2 * i // PER_BATCH)
                if from_(i, 2):
                    ranks(i - 2)
                attend(2 * i - 1, 1, (2 * i - 2) // PER_BATCH)

            pe.wait_ge(a_used, PAIRS - 1)
            pe.wait_ge(fsilu_ready, B * (FF // P))
            pe.wait_ge(fh_ready, B * (FF // P) - 1)
            scores(0, 0)
            down(B - 1)
            scores(1, 0)
            pe.wait_ge(ld_wo, 16)
            for g in range(6):
                b, c4 = divmod(g, 3)
                if g == 1:
                    pe.wait_ge(ff_added, B)
                if g == 3:
                    scores(2, 0)
                if g == 5:
                    pe.wait_ge(vo_used, 3)
                for c in range(4 * c4, min(4 * c4 + 4, CH)):
                    crossed = [p for p in range(PAIRS) if 0 < P + P * c - 2 * J * p < P + 2 * J]
                    for p in crossed:
                        at = P + P * c - 2 * J * p
                        last = nc.tensor.matmul(VO_PS[g][:, (c - 4 * c4) * P:(c - 4 * c4 + 1) * P],
                                                vpad[:, b, at:at + P], WO[:, p, :],
                                                start=p == crossed[0], stop=p == crossed[-1])
                last.then_inc(vo_ready, 1)
            pe.wait_ge(ld_gw, 32)
            pe.wait_ge(consts, 3)
            for i in range(1, PAIR_TURNS):
                pair_turn(i, begun=i == 1)
            attend(TILES - 2, 0, B - 1)
            attend(TILES - 1, 1, B - 1, PAIR_TURNS - 2)
            ranks(PAIR_TURNS - 2)
            keep_clock(8)
            transpose_y(PAIR_TURNS - 1)
            logits(PAIR_TURNS - 1)
            ranks(PAIR_TURNS - 1)

            pe.wait_ge(tables_ready, 1)
            keep_clock(12)
            pe.wait_ge(w_split, E)
            pe.wait_ge(ld_w2, 16)

            def transpose_slots(s, k, u):
                pe.wait_ge(rt_in[k], (s // RIN + 1) * 16)
                if from_(s, 1):
                    pe.wait_ge(s_split, s)
                nc.tensor.transpose(XP[:, 0:P], RT[:, k, 0:D], identf[:, :]).then_inc(sT_ready, 1)

            def slot_expert(s):
                return pe.value_load(expert_of[0:1, bass.ds(s, 1)], min_val=0, max_val=E - 1)

            def slot_gate_up(s, u, e):
                pe.wait_ge(s_split, s + 1)
                if from_(s, 2):
                    pe.wait_ge(he_ready, 2 * (s - 1))
                for n, (o, done) in enumerate(((GP, sgate_ready), (UP, sup_ready))):
                    cs = slice(n * F, (n + 1) * F)
                    mm3(o[u][:, :], XT_hi[u][:, :], XT_lo[u][:, :],
                        W13_hi[:, bass.ds(e, 1), cs].rearrange("p a f -> p (a f)"),
                        W13_lo[:, bass.ds(e, 1), cs].rearrange("p a f -> p (a f)")).then_inc(done, 1)

            held = [None]

            def slot_turn(s, k, u):
                e = held[0]
                e_next = held[0] = slot_expert(s + 1) if slots_ahead(s, 1) else None
                if from_(s, 2):
                    pe.wait_ge(heT_copied, s - 1)
                for c in range(FC):
                    if c % (FC // 2) == 0:
                        pe.wait_ge(he_ready, 2 * s + 1 + c // (FC // 2))
                    last = nc.tensor.transpose(HP[u][:, c * P:(c + 1) * P], HH[:, u, c * P:(c + 1) * P], identf[:, :])
                last.then_inc(heT_ready, 1)
                if slots_ahead(s, 1):
                    slot_gate_up(s + 1, 1 - u, e_next)
                if slots_ahead(s, 2):
                    transpose_slots(s + 2, (k + 2) % RIN, u)
                if k == 0:
                    e = slot_expert(s)
                pe.wait_ge(heT_copied, s + 1)
                if from_(s, 1):
                    pe.wait_ge(yo_ready, s)
                for c in range(FC):
                    last = nc.tensor.matmul(DP[:, 0:D], HT[:, u, c, :],
                                            W2[:, bass.ds(e, 1), c * P:(c + 1) * P].rearrange("p a f -> p (a f)"),
                                            start=c == 0, stop=c == FC - 1)
                last.then_inc(ye_ready, 1)

            transpose_slots(0, 0, 0)
            slot_gate_up(0, 0, slot_expert(0))
            transpose_slots(1, 1, 1)
            slot_loop(pe, slot_turn)


_INS = ['x', 'ctx_1024', 'g_xattn', 'g_ffn', 'L0_xattn_ln_g', 'L0_xattn_ln_b', 'L0_xattn_cln_g', 'L0_xattn_cln_b',
        'L0_xattn_Wq', 'L0_xattn_Wkv', 'L0_xattn_Wo', 'L0_xattn_Wff1', 'L0_xattn_Wff2', 'L0_ffn_gate_w',
        'L0_ffn_gate_b', 'L0_ffn_w1', 'L0_ffn_w3', 'L0_ffn_w2']
_OUTS = [((2, 512, 128), 'float32')]


def kernel(**inputs):
    import numpy as _np
    import concourse.bacc as _bacc
    from concourse import mybir as _mybir
    from concourse.bass_utils import run_bass_kernel_spmd as _run

    nc = _bacc.Bacc("TRN2", target_bir_lowering=False, num_devices=1)
    arrays, args = {}, []
    for name in _INS:
        a = _np.ascontiguousarray(inputs[name])
        arrays[f"in_{name}_dram"] = a
        args.append(nc.dram_tensor(f"in_{name}_dram", a.shape, _mybir.dt.from_np(a.dtype), kind="ExternalInput").ap())
    for i, (shape, dtype) in enumerate(_OUTS):
        dt = _mybir.dt.from_np(_np.dtype(dtype))
        args.append(nc.dram_tensor(f"out_{i}_dram", shape, dt, kind="ExternalOutput").ap())
    gated_block_kernel(nc, *args)
    r = _run(nc, [arrays], core_ids=[0])
    return r.results[0]["out_0_dram"]
```
